# Optimizing a Trainium2 kernel written in Bass

```python
import numpy as np
import jax
import jax.numpy as jnp

def _softmax(x, axis=-1):
    return jax.nn.softmax(x, axis=axis)

def _gelu(x):
    return jax.nn.gelu(x, approximate=True)

def _silu(x):
    return jax.nn.silu(x)

def _sigmoid(x):
    return jax.nn.sigmoid(x)

def _layernorm(x, axis=-1, eps=1e-05):
    m = jnp.mean(x, axis=axis, keepdims=True)
    v = jnp.var(x, axis=axis, keepdims=True)
    return (x - m) / jnp.sqrt(v + eps)

def _scatter_add(tgt, idx, src, axis=0):
    return tgt.at[idx].add(src)

def _segment_sum(src, seg, n):
    return jax.ops.segment_sum(src, seg, n)
kernel_name = 'mk_adj_ffn_d1_adj_r2_3ee162'

def setup_inputs(seed: int=0):
    np.random.seed(seed)
    _w = jnp.asarray

    def _rec_inputs():
        import jax
        import jax.numpy as jnp
        _gk = jax.random.key(seed)
        x = -0.0002928 + 1 * jax.random.normal(jax.random.fold_in(_gk, 1), (2048, 512), jnp.float32)
        _w = (1.0 + jnp.arange(2048, dtype=jnp.float32)) ** (-0.5)
        _w = _w / _w.mean()
        _pij = jnp.clip(0.00390625 * _w[:, None] * _w[None, :], 0.0, 1.0)
        _a = jax.random.uniform(jax.random.fold_in(_gk, 2), (2048, 2048)) < _pij
        _af = _a.astype(jnp.float32)
        adj = _af
        return (x, adj)
    x, adj = _rec_inputs()

    def _L0_gnn_setup():
        import jax, jax.numpy as jnp
        import numpy as np
        N = 2048
        D_IN = 512
        H = 16
        DH = D_IN // H
        ALPHA = 0.2
        MASK_VAL = -65500.0
        key = jax.random.key(seed)
        ks = jax.random.split(key, 7)
        x = jax.random.normal(ks[0], (N, D_IN), dtype=jnp.float32)
        adj = jax.random.randint(ks[1], (N, N), 0, 2).astype(jnp.float32)
        s = 1.0 / np.sqrt(D_IN)
        W_seq = jax.random.normal(ks[2], (D_IN, D_IN), dtype=jnp.float32) * s
        a1 = jax.random.normal(ks[3], (DH,), dtype=jnp.float32) / np.sqrt(DH)
        a2 = jax.random.normal(ks[4], (DH,), dtype=jnp.float32) / np.sqrt(DH)
        W_out = jax.random.normal(ks[5], (D_IN, D_IN), dtype=jnp.float32) * s
        b_out = jax.random.normal(ks[6], (D_IN,), dtype=jnp.float32) * 0.01
        return {'x': x, 'adj': adj, 'W_seq': W_seq, 'a1': a1, 'a2': a2, 'W_out': W_out, 'b_out': b_out}
    _L0_gnn_all = _L0_gnn_setup()
    _L0_gnn_in = {k: v for k, v in _L0_gnn_all.items() if k in ('W_seq', 'a1', 'a2', 'W_out', 'b_out')}
    del _L0_gnn_all

    def _L0_ffn_setup():
        import jax, jax.numpy as jnp
        import numpy as np
        B, S, D = (4, 1024, 512)
        E, H, K = (8, 1024, 2)
        key = jax.random.key(seed)
        k_x, k_g, k1, k2, k3 = jax.random.split(key, 5)
        x = jax.random.normal(k_x, (B, S, D), dtype=jnp.float32)
        Wg = jax.random.normal(k_g, (E, D), dtype=jnp.float32) * 0.02
        W1 = jax.random.normal(k1, (E, H, D), dtype=jnp.float32) * 0.02
        W2 = jax.random.normal(k2, (E, H, D), dtype=jnp.float32) * 0.02
        W3 = jax.random.normal(k3, (E, D, H), dtype=jnp.float32) * 0.02
        return {'x': x, 'Wg': Wg, 'W1': W1, 'W2': W2, 'W3': W3}
    _L0_ffn_all = _L0_ffn_setup()
    _L0_ffn_in = {k: v for k, v in _L0_ffn_all.items() if k in ('Wg', 'W1', 'W2', 'W3')}
    del _L0_ffn_all
    return {'x': x, 'adj': adj, 'L0_gnn_W_seq': _L0_gnn_in['W_seq'], 'L0_gnn_a1': _L0_gnn_in['a1'], 'L0_gnn_a2': _L0_gnn_in['a2'], 'L0_gnn_W_out': _L0_gnn_in['W_out'], 'L0_gnn_b_out': _L0_gnn_in['b_out'], 'L0_ffn_Wg': _L0_ffn_in['Wg'], 'L0_ffn_W1': _L0_ffn_in['W1'], 'L0_ffn_W2': _L0_ffn_in['W2'], 'L0_ffn_W3': _L0_ffn_in['W3']}

def reference(x, adj, L0_gnn_W_seq, L0_gnn_a1, L0_gnn_a2, L0_gnn_W_out, L0_gnn_b_out, L0_ffn_Wg, L0_ffn_W1, L0_ffn_W2, L0_ffn_W3):
    import jax
    import jax.numpy as jnp

    def _L0_gnn_ref(x, adj, W_seq, a1, a2, W_out, b_out):
        import jax, jax.numpy as jnp
        import numpy as np
        N = 2048
        D_IN = 512
        H = 16
        DH = D_IN // H
        ALPHA = 0.2
        MASK_VAL = -65500.0
        seq = (x @ W_seq).reshape(N, H, DH)
        score1 = jnp.einsum('nhd,d->hn', seq, a1)
        score2 = jnp.einsum('nhd,d->hn', seq, a2)
        scores = score1[:, :, None] + score2[:, None, :]
        scores = jax.nn.leaky_relu(scores, negative_slope=ALPHA)
        scores = scores + (1.0 - adj)[None, :, :] * MASK_VAL
        attn = jax.nn.softmax(scores, axis=-1)
        hidden = jnp.einsum('hij,jhd->ihd', attn, seq).reshape(N, D_IN)
        hidden = hidden @ W_out + b_out
        return jax.nn.elu(hidden)

    def _L0_ffn_ref(x, Wg, W1, W2, W3):
        import jax, jax.numpy as jnp
        import numpy as np
        B, S, D = (4, 1024, 512)
        E, H, K = (8, 1024, 2)
        scores = jnp.einsum('bsd,ed->bse', x, Wg)
        topk_scores, topk_idx = jax.lax.top_k(scores, K)
        topk_probs = jax.nn.softmax(topk_scores, axis=-1)
        gating = jnp.sum(jax.nn.one_hot(topk_idx, E, dtype=x.dtype) * topk_probs[..., None], axis=-2)
        h1 = jnp.einsum('bsd,ehd->bseh', x, W1)
        h2 = jnp.einsum('bsd,ehd->bseh', x, W2)
        hidden = jax.nn.silu(h1) * h2
        expert_out = jnp.einsum('bseh,edh->bsed', hidden, W3)
        y = jnp.einsum('bse,bsed->bsd', gating, expert_out)
        return y
    x = x + _L0_gnn_ref(_layernorm(x, axis=-1), adj, L0_gnn_W_seq, L0_gnn_a1, L0_gnn_a2, L0_gnn_W_out, L0_gnn_b_out)
    x = x + _L0_ffn_ref(_layernorm(x, axis=-1)[None], L0_ffn_Wg, L0_ffn_W1, L0_ffn_W2, L0_ffn_W3)[0]
    return x

_drawn_inputs = setup_inputs


def setup_inputs(seed=0):
    import zlib

    import numpy as np

    out = dict(_drawn_inputs(seed))
    spreads = {}
    factors = {'L0_gnn_b_out': 6.431}
    for name, (base, spread) in spreads.items():
        noise = np.random.default_rng([zlib.crc32(name.encode()), seed]).standard_normal(out[name].shape)
        drawn = base * np.exp(spread * noise) if base else spread * noise
        out[name] = jnp.asarray(drawn.astype(out[name].dtype))
    for name, factor in factors.items():
        out[name] = (out[name] * factor).astype(out[name].dtype)
    return out
```

```python
import concourse.bass as bass
from concourse import mybir
from contextlib import ExitStack

F32 = mybir.dt.float32
F32R = mybir.dt.float32r
BF16 = mybir.dt.bfloat16
I32 = mybir.dt.int32
ALU = mybir.AluOpType
ACT = mybir.ActivationFunctionType
AX = mybir.AxisListType

P = 128
N, D = 2048, 512
H, DH = 16, 32
E, HID = 8, 1024
KT = D // P
NT = N // P
CH = 512
NC = N // CH
TPC = CH // P
Q = DH + 1
Q2 = 2 * Q
PARTS = 3
EPS = 1e-5
BIG = float(2 ** 60)

HB = 4
NG = H // HB
BJ = 4
NB = NT // BJ
ON_ACT = [3, 3, 3, 4]

UN = E * HID // P
GH = 2
GPE = HID // P // GH
GROUPS = UN // GH
WU = 2 * KT * P + D


def build(nc, x, adjT, W_seq, a1, a2, W_out, b_out, WgT, ffn_w, out):
    ctx = ExitStack()
    with ctx:
        def keep(name, shape, dt, where=None):
            return (where or ctx).enter_context(nc.sbuf_tensor(name, shape, dt))

        def sem(name):
            return ctx.enter_context(nc.semaphore(name))

        s1_rows = nc.dram_tensor("s1_rows", [NC * H, CH], F32, kind="Internal").ap()
        x2_dram = nc.dram_tensor("x2_dram", [NT, P, D], F32, kind="Internal").ap()
        xh_dram = nc.dram_tensor("xh_dram", [NC, P, KT, CH], F32, kind="Internal").ap()
        xl_dram = nc.dram_tensor("xl_dram", [NC, P, KT, CH], F32, kind="Internal").ap()

        ident = keep("ident", [P, P], F32)
        ones = keep("ones", [P, P], F32)
        ones_bf = keep("ones_bf", [P, P], BF16)
        wg = keep("wg", [P, KT, E], F32)
        wg_hi = keep("wg_hi", [P, KT, E], F32R)
        wg_lo = keep("wg_lo", [P, KT, E], F32R)
        gates = keep("gates", [P, NT, E], F32)
        minus_half = keep("minus_half", [P, TPC], F32)

        bank = [ctx.enter_context(nc.psum_tensor(f"bank{i}", [P, 512], F32)) for i in range(8)]

        A = ExitStack()
        adj = keep("adj", [P, 2, NT, CH], BF16, A)
        X0 = ExitStack()
        xall = keep("xall", [P, NT, D], F32, X0)
        wtmp = keep("wtmp", [P, KT * H, DH], F32, X0)
        a_rows = keep("a_rows", [P, 2, DH], F32, X0)
        X0.close()
        uv = keep("uv", [P, NT, H, PARTS * Q2], BF16, A)
        s2_big = keep("s2_big", [P, NT, H], F32, A)
        s2_neg = keep("s2_neg", [P, NT, H], F32, A)
        row_a = keep("row_a", [P, NT, H], F32, A)
        row_c = keep("row_c", [P, NT, H], F32, A)
        w_out = keep("w_out", [P, KT, D], F32, A)
        b_row = keep("b_row", [P, D], F32, A)
        X1 = ExitStack()
        xT = keep("xT", [P, KT, N], F32, X1)
        w_seq = keep("w_seq", [P, KT, D], F32, X1)
        w12 = keep("w12", [P, KT, 2 * H], F32, X1)
        s21T = keep("s21T", [2 * H, N], F32, X1)
        gmax = keep("gmax", [H, 1], F32, X1)
        gdiag = keep("gdiag", [H, H], F32, X1)
        gcol = keep("gcol", [P, H], F32, X1)
        col_B = keep("col_B", [P, NT, H], F32, X1)
        col_D = keep("col_D", [P, NT, H], F32, X1)
        y_col = keep("y_col", [P, NT, H], F32, X1)
        ylo = keep("ylo", [P, NT, H], F32, X1)
        s2c = keep("s2c", [P, NT, H], F32, X1)
        uvf = keep("uvf", [P, 2, H, Q2], F32, X1)
        bst0 = keep("bst0", [P, NT, 6], F32, X1)
        mv0 = keep("mv0", [P, NT, 2], F32, X1)
        rs0 = keep("rs0", [P, 4, NT], F32, X1)
        X1.close()
        s1_bc = keep("s1_bc", [P, HB, CH], F32, A)
        mask = keep("mask", [P, NB, BJ, CH], BF16, A)
        sums = keep("sums", [P, TPC * H, Q2], F32, A)
        av = keep("av", [P, TPC * H, Q], F32, A)
        empty = keep("empty", [P, CH], BF16, A)
        rden = keep("rden", [P, TPC * H], F32, A)
        hid = keep("hid", [P, D], F32, A)
        hidT = keep("hidT", [P, KT, P], F32, A)
        z = keep("z", [P, D], F32, A)
        ez = keep("ez", [P, D], F32, A)
        xt = keep("xt", [P, D], F32, A)
        xn = keep("xn", [P, D], F32, A)
        xh = keep("xh", [P, KT, P], F32R, A)
        xl = keep("xl", [P, KT, P], F32R, A)
        bst = keep("bst", [P, 6], F32, A)
        mv = keep("mv", [P, 2], F32, A)
        rs = keep("rs", [P, 4], F32, A)
        A.close()

        B = ctx
        w_hi = keep("w_hi", [P, 2, GH, WU], F32R, B)
        w_lo = keep("w_lo", [P, 2, GH, WU], F32R, B)
        w_raw = keep("w_raw", [P, 2, WU], F32, B)
        h_hi = keep("h_hi", [P, 2, GH, CH], F32R, B)
        h_lo = keep("h_lo", [P, 2, GH, CH], F32R, B)
        act_s = keep("act_s", [P, GH, CH], F32, B)
        act_g = keep("act_g", [P, GH, CH], F32, B)
        XH = [keep(f"XH{c}", [P, KT, CH], F32R, B) for c in range(NC)]
        XL = [keep(f"XL{c}", [P, KT, CH], F32R, B) for c in range(NC)]
        acc = keep("acc", [P, NT, D], F32, B)
        sc = keep("sc", [P, NT, E], F32, B)
        eq1 = keep("eq1", [P, NT, E], F32, B)
        eq2 = keep("eq2", [P, NT, E], F32, B)
        rank = keep("rank", [P, E], F32, B)
        top = keep("top", [P, 6, NT], F32, B)

        x_in = [sem(f"x_in{i}") for i in range(4)]
        w_in = sem("w_in")
        wo_in = sem("wo_in")
        s1_out = sem("s1_out")
        adj_in = [sem(f"adj_in{i}") for i in range(2)]
        s1_in = [sem(f"s1_in{i}") for i in range(HB)]
        xt_in = sem("xt_in")
        tok_out = sem("tok_out")
        raw_in = [sem(f"raw_in{i}") for i in range(2)]
        XT_in = [sem(f"XT_in{c}") for c in range(NC)]
        acc_in = sem("acc_in")
        out_done = sem("out_done")
        const_ok = sem("const_ok")
        su_dve = sem("su_dve")
        su_act = sem("su_act")
        su_pool = sem("su_pool")
        su_tr = sem("su_tr")
        su_xT = sem("su_xT")
        su_sT = sem("su_sT")
        su_sTc = sem("su_sTc")
        su_cols = sem("su_cols")
        su_g = sem("su_g")
        seq_ready = sem("seq_ready")
        seq_used = sem("seq_used")
        uvf_ready = sem("uvf_ready")
        hi_ready = sem("hi_ready")
        rest_ready = sem("rest_ready")
        mid_ready = sem("mid_ready")
        uv_ready = sem("uv_ready")
        held = sem("held")
        relu_ready = sem("relu_ready")
        mask_ready = sem("mask_ready")
        batch_done = sem("batch_done")
        sums_free = sem("sums_free")
        av_ready = sem("av_ready")
        av_free = sem("av_free")
        deg_ready = sem("deg_ready")
        empty_ready = sem("empty_ready")
        adj_ok = sem("adj_ok")
        comb = sem("comb")
        tok_dve = sem("tok_dve")
        tok_tr1 = sem("tok_tr1")
        tok_hidT = sem("tok_hidT")
        tok_proj = sem("tok_proj")
        tok_exp = sem("tok_exp")
        tok_rs = sem("tok_rs")
        tok_tr2 = sem("tok_tr2")
        tok_xh = sem("tok_xh")
        w_hi_ok = sem("w_hi_ok")
        w_lo_ok = sem("w_lo_ok")
        h1_ready = sem("h1_ready")
        h2_ready = sem("h2_ready")
        silu_ready = sem("silu_ready")
        g_ready = sem("g_ready")
        hi_done = sem("hi_done")
        hid_ready = sem("hid_ready")
        y_ready = sem("y_ready")
        y_used = sem("y_used")
        sc_ready = sem("sc_ready")
        gate_dve = sem("gate_dve")
        gate_exp = sem("gate_exp")

        S_HID, S_Z, S_NEG, S_ELU, S_X2, S_BN, S_MV, S_VE, S_N1, S_N2, S_RS, S_XN, S_XL = range(1, 14)
        S_ALL = 13
        C_ALL = 5
        DEG_BANK = 6
        TR, PR = bank[6], bank[7]

        block = ctx.enter_context(nc.Block())

        SU_VAR, SU_XN, SU_DIAG, SU_COLS = [0] * 4, [0] * NT, [0], [0]
        GATE_EXP = 13

        SU = [0]

        def setup_vector(dve):
            def step(ins, wait=None):
                ins.then_inc(su_dve, 1)
                SU[0] += 1
                return SU[0]

            def settle():
                dve.wait_ge(su_dve, SU[0])

            dve.wait_ge(w_in, 64)
            wv = w_seq[:].rearrange("p k (h d) -> p (k h) d", d=DH)
            for s in range(2):
                settle()
                step(nc.vector.tensor_tensor(wtmp[:], wv, a_rows[:, 1 - s, :].unsqueeze(1).broadcast_to([P, KT * H, DH]),
                                             ALU.mult))
                settle()
                step(nc.vector.tensor_reduce(w12[:, :, s * H:(s + 1) * H],
                                             wtmp[:].rearrange("p (k h) d -> p k h d", k=KT),
                                             axis=AX.X, op=ALU.add))
            step(nc.vector.tensor_copy(wg_hi[:], wg[:]))
            settle()
            step(nc.vector.tensor_tensor(wg_lo[:], wg[:], wg_hi[:].bitcast(F32), ALU.subtract))
            for q in range(4):
                dve.wait_ge(x_in[q], 16)
                ts = range(4 * q, 4 * q + 4)
                for t in ts:
                    step(nc.vector.bn_stats(bst0[:, t, :], xall[:, t, :]))
                settle()
                for t in ts:
                    step(nc.vector.bn_aggr(mv0[:, t, :], bst0[:, t, :]))
                settle()
                qs = slice(4 * q, 4 * q + 4)
                SU_VAR[q] = step(nc.vector.tensor_scalar(rs0[:, 0, qs], mv0[:, qs, 1], EPS, None, ALU.add))
                dve.wait_ge(su_pool, 5 + q)
                newton(dve, rs0[:, 0, qs], rs0[:, 1, qs], rs0[:, 2, qs], step, settle)
                settle()
                for t in ts:
                    SU_XN[t] = step(nc.vector.tensor_scalar(xall[:, t, :], xall[:, t, :], mv0[:, t, 0:1],
                                                            rs0[:, 1, t:t + 1], ALU.subtract, ALU.mult))
            dve.wait_ge(su_sTc, NC)
            step(nc.vector.reduce_max(gmax[:], s21T[0:H, :], axis=AX.X))
            settle()
            SU_DIAG[0] = step(nc.vector.tensor_scalar(gdiag[:], ident[0:H, 0:H], gmax[:, 0:1], None, ALU.mult))
            dve.wait_ge(su_g, 1)
            step(nc.vector.tensor_copy(gcol[:], bank[1][:, 0:H]))
            settle()
            gb = gcol[:].unsqueeze(1).broadcast_to([P, NT, H])
            cols = bank[0][:].rearrange("p (t s) -> p t s", t=NT)
            dve.wait_ge(su_cols, 1)
            step(nc.vector.tensor_tensor(s2c[:], cols[:, :, 0:H], gb, ALU.subtract))
            step(nc.vector.tensor_tensor(y_col[:], cols[:, :, H:2 * H], gb, ALU.add))
            step(nc.vector.tensor_scalar(s2_big[:], cols[:, :, 0:H], BIG, None, ALU.mult))
            step(nc.vector.tensor_scalar(s2_neg[:], cols[:, :, 0:H], -1.0, None, ALU.mult))
            settle()
            step(nc.vector.tensor_scalar(ylo[:], y_col[:], 0.0, None, ALU.min))
            settle()
            SU_COLS[0] = step(nc.vector.tensor_scalar(y_col[:], y_col[:], 0.0, None, ALU.max))

        def newton(dve, v, y, t, step, settle):
            step(nc.vector.tensor_tensor(t, y, y, ALU.mult))
            settle()
            step(nc.vector.tensor_tensor(t, t, v, ALU.mult))
            settle()
            step(nc.vector.tensor_scalar(t, t, -0.5, 1.5, ALU.mult, ALU.add))
            settle()
            step(nc.vector.tensor_tensor(y, y, t, ALU.mult))

        @block.vector
        def _(dve):
            dve.wait_ge(const_ok, 1)
            setup_vector(dve)
            dve.wait_ge(su_act, 4)
            ends = 0

            def rest(t):
                u = uvf[:, t % 2]
                dve.wait_ge(hi_ready, t + 1)
                nc.vector.tensor_tensor(u, u, uv[:, t, :, 0:Q2], ALU.subtract).then_inc(rest_ready, 1)

            def low(t):
                dve.wait_ge(mid_ready, t + 1)
                nc.vector.tensor_tensor(uv[:, t, :, 2 * Q2:], uvf[:, t % 2], uv[:, t, :, Q2:2 * Q2],
                                        ALU.subtract).then_inc(uv_ready, 1)

            for t in range(NT):
                u = uvf[:, t % 2]
                dve.wait_ge(seq_ready, t + 1)
                if t >= 2:
                    dve.wait_ge(uv_ready, t - 1)
                sq = bank[2 + t % 2][:].rearrange("p (h d) -> p h d", d=DH)
                for s, f in ((0, col_B), (1, col_D)):
                    last = nc.vector.tensor_tensor(u[:, :, s * Q:s * Q + DH], sq,
                                                   f[:, t, :].unsqueeze(2).broadcast_to([P, H, DH]), ALU.mult)
                last.then_inc(seq_used, 1)
                for s, f in ((0, col_B), (1, col_D)):
                    last = nc.vector.tensor_copy(u[:, :, s * Q + DH], f[:, t, :])
                last.then_inc(uvf_ready, 1)
                if t >= 1:
                    low(t - 1)
                rest(t)
            low(NT - 1)

            def fix_adj(c):
                dve.wait_ge(deg_ready, c + 1)
                nc.vector.tensor_scalar(empty[:], bank[DEG_BANK][:], 0.0, None, ALU.is_equal).then_inc(empty_ready, 1)
                dve.wait_ge(empty_ready, c + 1)
                for q in range(4):
                    a = adj[:, c % 2, 4 * q:4 * q + 4, :]
                    nc.vector.tensor_tensor(a, a, empty[:].unsqueeze(1).broadcast_to([P, 4, CH]),
                                            ALU.add).then_inc(adj_ok, 1)
                dve.wait_ge(adj_ok, 4 * (c + 1))

            def masks(c, g, hh, b):
                it = NG * c + g
                n = NB * (HB * it + hh) + b
                dve.wait_ge(relu_ready, n + 1)
                k = ON_ACT[b]
                m = mask[:, b, 0:k, :]
                last = nc.vector.tensor_tensor(m, m, adj[:, c % 2, BJ * b:BJ * b + k, :], ALU.min)
                for k in range(ON_ACT[b], BJ):
                    j = BJ * b + k
                    last = nc.vector.scalar_tensor_tensor(mask[:, b, k, :], s1_bc[:, hh, :],
                                                          s2_neg[:, j, bass.ds(HB * g + hh, 1)],
                                                          adj[:, c % 2, j, :], ALU.is_gt, ALU.mult)
                last.then_inc(mask_ready, 1)

            def take_sums(c, g, hh):
                it = NG * c + g
                dve.wait_ge(const_ok, 1)
                dve.wait_ge(batch_done, NB * (HB * it + hh + 1) + NB)
                sv = sums[:].rearrange("p (t h) q -> p t h q", h=H)
                for q in range(2):
                    last = nc.vector.tensor_reduce(
                        sv[:, 2 * q:2 * q + 2, bass.ds(HB * g + hh, 1), :].rearrange("p t o q -> p (t o) q"),
                        bank[2 * (hh % 2) + q][:, 0:2 * PARTS * Q2].rearrange("p (t r q) -> p t q r", t=2, r=PARTS),
                        axis=AX.X, op=ALU.add)
                last.then_inc(sums_free, 1)

            def take_av(c, g, q):
                it = NG * c + g
                dve.wait_ge(const_ok, 1)
                dve.wait_ge(av_ready, NG * it + q + 1)
                vv = av[:].rearrange("p (t h) q -> p t h q", h=H)
                nc.vector.tensor_reduce(
                    vv[:, bass.ds(g, 1), HB * q:HB * (q + 1), :].rearrange("p o h q -> p (o h) q"),
                    bank[4 + q % 2][:, 0:HB * PARTS * Q].rearrange("p (h r q) -> p h q r", h=HB, r=PARTS),
                    axis=AX.X, op=ALU.add).then_inc(av_free, 1)

            def combine(c):
                n = C_ALL * c
                ra = row_a[:, TPC * c:TPC * (c + 1), :].rearrange("p t h -> p (t h)").unsqueeze(2) \
                    .broadcast_to([P, TPC * H, Q])
                rc = row_c[:, TPC * c:TPC * (c + 1), :].rearrange("p t h -> p (t h)").unsqueeze(2) \
                    .broadcast_to([P, TPC * H, Q])
                dve.wait_ge(sums_free, H * (c + 1) + 2)
                dve.wait_ge(av_free, NG * NG * (c + 1) + 2)
                nc.vector.tensor_tensor(av[:], av[:], sums[:, :, Q:Q2], ALU.subtract).then_inc(comb, 1)
                nc.vector.tensor_tensor(sums[:, :, 0:Q], sums[:, :, 0:Q], ra, ALU.mult).then_inc(comb, 1)
                dve.wait_ge(comb, n + 1)
                nc.vector.tensor_tensor(av[:], av[:], rc, ALU.mult).then_inc(comb, 1)
                dve.wait_ge(comb, n + 3)
                nc.vector.tensor_tensor(av[:], av[:], sums[:, :, 0:Q], ALU.add).then_inc(comb, 1)
                dve.wait_ge(comb, n + 4)
                nc.vector.reciprocal(rden[:], av[:, :, DH]).then_inc(comb, 1)
                dve.wait_ge(comb, n + 5)

            def tok_hid(T, g):
                vv = av[:].rearrange("p (t h) q -> p t h q", h=H)[:, bass.ds(g, 1), :, 0:DH] \
                    .rearrange("p o h q -> p (o h) q")
                rv = rden[:].rearrange("p (t h) -> p t h", h=H)[:, bass.ds(g, 1), :].rearrange("p o h -> p (o h)")
                dve.wait_ge(tok_tr1, T + 1)
                nc.vector.tensor_tensor(hid[:].rearrange("p (h q) -> p h q", q=DH), vv,
                                        rv.unsqueeze(2).broadcast_to([P, H, DH]), ALU.mult).then_inc(tok_dve, 1)

            def tok_z(T):
                dve.wait_ge(tok_proj, T + 1)
                nc.vector.tensor_tensor(z[:], PR[:], b_row[:], ALU.add).then_inc(tok_dve, 1)
                dve.wait_ge(tok_dve, S_ALL * T + S_Z)
                nc.vector.tensor_scalar(ez[:], z[:], 0.0, None, ALU.min).then_inc(tok_dve, 1)

            def tok_x2(T):
                n = S_ALL * T
                dve.wait_ge(tok_exp, T + 1)
                nc.vector.scalar_tensor_tensor(ez[:], z[:], 0.0, ez[:], ALU.max, ALU.add).then_inc(tok_dve, 1)
                dve.wait_ge(tok_dve, n + S_ELU)
                dve.wait_ge(xt_in, 16 * (T + 1))
                nc.vector.scalar_tensor_tensor(xt[:], ez[:], -1.0, xt[:], ALU.add, ALU.add).then_inc(tok_dve, 1)
                dve.wait_ge(tok_dve, n + S_X2)
                nc.vector.bn_stats(bst[:], xt[:]).then_inc(tok_dve, 1)
                dve.wait_ge(tok_dve, n + S_BN)
                dve.sem_inc(held, 1)
                nc.vector.bn_aggr(mv[:], bst[:]).then_inc(tok_dve, 1)
                dve.wait_ge(tok_dve, n + S_MV)
                nc.vector.tensor_scalar(rs[:, 0:1], mv[:, 1:2], EPS, None, ALU.add).then_inc(tok_dve, 1)

            def tok_norm(T):
                n = S_ALL * T
                dve.wait_ge(tok_rs, T + 1)
                nc.vector.scalar_tensor_tensor(rs[:, 2:3], rs[:, 1:2], rs[:, 1:2], rs[:, 0:1],
                                               ALU.mult, ALU.mult).then_inc(tok_dve, 1)
                dve.wait_ge(tok_dve, n + S_N1)
                nc.vector.tensor_scalar(rs[:, 2:3], rs[:, 2:3], -0.5, 1.5, ALU.mult, ALU.add).then_inc(tok_dve, 1)
                dve.wait_ge(tok_dve, n + S_N2)
                nc.vector.tensor_tensor(rs[:, 3:4], rs[:, 1:2], rs[:, 2:3], ALU.mult).then_inc(tok_dve, 1)
                dve.wait_ge(tok_dve, n + S_RS)
                nc.vector.tensor_scalar(xn[:], xt[:], mv[:, 0:1], rs[:, 3:4], ALU.subtract, ALU.mult).then_inc(tok_dve, 1)

            def tok_low(T):
                dve.wait_ge(tok_xh, T + 1)
                nc.vector.tensor_tensor(xl[:], TR[:].rearrange("p (k i) -> p k i", k=KT), xh[:].bitcast(F32),
                                        ALU.subtract).then_inc(tok_dve, 1)

            for c in range(NC):
                fix_adj(c)
                with dve.Fori(0, NG) as g:
                    T = NG * (c - 1) + g
                    ep = c > 0
                    if ep:
                        tok_hid(T, g)
                    for hh in range(HB):
                        for b in range(NB):
                            masks(c, g, hh, b)
                            if b == 1 and hh > 0:
                                take_sums(c, g, hh - 1)
                            if (hh, b) == (1, 2):
                                take_av(c, g, 0)
                                take_av(c, g, 1)
                            if (hh, b) == (1, 3) and ep:
                                tok_z(T)
                            if (hh, b) == (3, 0) and ep:
                                tok_x2(T)
                            if (hh, b) == (3, 2):
                                take_av(c, g, 2)
                                take_av(c, g, 3)
                                if ep:
                                    tok_norm(T)
                    take_sums(c, g, HB - 1)
                    if ep:
                        tok_low(T)
                combine(c)
            for g in range(TPC):
                T = NT - TPC + g
                tok_hid(T, g)
                tok_z(T)
                tok_x2(T)
                tok_norm(T)
                tok_low(T)

            def split_lo(u, s, par):
                dve.wait_ge(w_hi_ok, u + 1)
                nc.vector.tensor_tensor(w_lo[:, par, s, :], w_raw[:, s, :], w_hi[:, par, s, :].bitcast(F32),
                                        ALU.subtract).then_inc(w_lo_ok, 1)

            dve.wait_ge(tok_out, 48 * NT + 16)
            split_lo(0, 0, 0)
            split_lo(1, 1, 0)

            dve.wait_ge(sc_ready, 1)
            G = [0]

            def gstep(ins):
                ins.then_inc(gate_dve, 1)
                G[0] += 1
                dve.wait_ge(gate_dve, G[0])
            b8 = lambda r: top[:, r, :].unsqueeze(2).broadcast_to([P, NT, E])
            dve.wait_ge(const_ok, 1 + E)
            rk = rank[:].unsqueeze(1).broadcast_to([P, NT, E])
            gstep(nc.vector.tensor_copy(sc[:], bank[4][:, 0:NT * E].rearrange("p (t e) -> p t e", e=E)))
            gstep(nc.vector.tensor_reduce(top[:, 0, :], sc[:], axis=AX.X, op=ALU.max))
            for r, eq in ((0, eq1), (1, eq2)):
                gstep(nc.vector.tensor_tensor(eq[:], sc[:], b8(r), ALU.is_equal))
                gstep(nc.vector.tensor_tensor(eq[:], eq[:], rk, ALU.mult))
                gstep(nc.vector.tensor_reduce(top[:, 3, :], eq[:], axis=AX.X, op=ALU.max))
                gstep(nc.vector.tensor_tensor(eq[:], eq[:], b8(3), ALU.is_equal))
                if r == 0:
                    gstep(nc.vector.scalar_tensor_tensor(sc[:], eq[:], -3.0e38, sc[:], ALU.mult, ALU.add))
                    gstep(nc.vector.tensor_reduce(top[:, 1, :], sc[:], axis=AX.X, op=ALU.max))
            gstep(nc.vector.tensor_tensor(top[:, 2, :], top[:, 1, :], top[:, 0, :], ALU.subtract))
            assert G[0] == GATE_EXP, G[0]
            dve.wait_ge(gate_exp, 1)
            gstep(nc.vector.tensor_scalar(top[:, 4, :], top[:, 2, :], 1.0, None, ALU.add))
            gstep(nc.vector.reciprocal(top[:, 4, :], top[:, 4, :]))
            gstep(nc.vector.tensor_tensor(top[:, 5, :], top[:, 2, :], top[:, 4, :], ALU.mult))
            gstep(nc.vector.tensor_tensor(eq1[:], eq1[:], b8(4), ALU.mult))
            gstep(nc.vector.tensor_tensor(eq2[:], eq2[:], b8(5), ALU.mult))
            gstep(nc.vector.tensor_tensor(gates[:], eq1[:], eq2[:], ALU.add))
            dve.wait_ge(acc_in, 16)

            def hidden(S, par):
                for ht in range(GH):
                    n = GH * S + ht
                    dve.wait_ge(silu_ready, n + 1)
                    dve.wait_ge(h2_ready, n + 1)
                    nc.vector.tensor_tensor(act_g[:, ht, :], act_s[:, ht, :], bank[2 * ht + 1][:],
                                            ALU.mult).then_inc(g_ready, 1)
                    dve.wait_ge(g_ready, n + 1 + GH)
                    dve.wait_ge(y_ready, TPC * (S + 1))
                    nc.vector.tensor_copy(h_hi[:, par, ht, :], act_g[:, ht, :]).then_inc(hi_done, 1)
                    dve.wait_ge(hi_done, n + 1)
                    nc.vector.tensor_tensor(h_lo[:, par, ht, :], act_g[:, ht, :], h_hi[:, par, ht, :].bitcast(F32),
                                            ALU.subtract).then_inc(hid_ready, 1)

            def take_y(S, c, e):
                for tt in range(TPC):
                    t = TPC * c + tt
                    dve.wait_ge(y_ready, TPC * S + tt + 1 + 2 * TPC)
                    nc.vector.scalar_tensor_tensor(acc[:, t, :], bank[4 + tt][:], gates[:, t, bass.ds(e, 1)],
                                                   acc[:, t, :], ALU.mult, ALU.add).then_inc(y_used, 1)

            hidden(0, 0)

            def two_groups(i, last):
                for k in range(2 * NC):
                    grp = 2 * i + k // NC
                    S = 2 * NC * i + k
                    if not (last and k == 2 * NC - 1):
                        hidden(S + 1, (k + 1) % 2)
                    take_y(S, k % NC, i // 2 if isinstance(i, int) else i // 2)
                    if k % NC < GH and not (last and k >= NC):
                        split_lo(GH * (grp + 1) + k % NC, k % NC, (k // NC + 1) % 2)

            with dve.Fori(0, GROUPS // 2 - 1) as i:
                two_groups(i, False)
            two_groups(GROUPS // 2 - 1, True)

        @block.sync
        def _(sp):
            sp.sem_inc(tok_out, 16)
            xv = x.rearrange("(t p) d -> p t d", p=P)
            for i in range(4):
                sp.dma_start(xall[:, 4 * i:4 * i + 4, :], xv[:, 4 * i:4 * i + 4, :]).then_inc(x_in[i], 16)
                if i == 0:
                    sp.dma_start(a_rows[:, 0, :], a1.partition_broadcast(P)).then_inc(w_in, 16)
                    sp.dma_start(a_rows[:, 1, :], a2.partition_broadcast(P)).then_inc(w_in, 16)
                    sp.dma_start(w_seq[:], W_seq.rearrange("(k p) n -> p k n", p=P)).then_inc(w_in, 16)
                    sp.dma_start(wg[:], WgT.rearrange("(k p) e -> p k e", p=P)).then_inc(w_in, 16)
            sp.dma_start(w_out[:], W_out.rearrange("(k p) n -> p k n", p=P)).then_inc(wo_in, 16)
            sp.dma_start(b_row[:], b_out.partition_broadcast(P)).then_inc(wo_in, 16)
            sp.wait_ge(su_sTc, NC)
            sp.dma_start(s1_rows.rearrange("(c h) i -> h c i", h=H),
                         s21T[H:2 * H, :].rearrange("h (c i) -> h c i", c=NC)).then_inc(s1_out, 16)
            sp.wait_ge(s1_out, 16)
            sp.wait_ge(uv_ready, NT)
            for hh in range(HB):
                sp.dma_start(s1_bc[:, hh, :], s1_rows[hh].partition_broadcast(P)).then_inc(s1_in[hh], 16)

            def step(c, g, tail):
                it = NG * c + g
                if c > 0:
                    T = it - NG
                    sp.wait_ge(tok_out, 48 * T + 16)
                    sp.sem_inc(held, 1)
                    sp.dma_start(xt[:], x.rearrange("(t p) d -> t p d", p=P)[T]).then_inc(xt_in, 16)
                if not tail:
                    for hh in range(HB):
                        sp.wait_ge(mask_ready, NB * (HB * it + hh + 1))
                        sp.sem_inc(held, 1)
                        sp.dma_start(s1_bc[:, hh, :], s1_rows[HB * (it + 1) + hh].partition_broadcast(P)) \
                          .then_inc(s1_in[hh], 16)
                if c > 0:
                    store_tile(T, c - 1, g)

            def store_tile(T, c, g):
                sp.wait_ge(tok_dve, S_ALL * T + S_XL)
                sp.sem_inc(held, 1)
                sp.wait_ge(tok_xh, T + 1)
                sp.sem_inc(held, 1)
                sp.dma_start(x2_dram[T], xt[:]).then_inc(tok_out, 16)
                sp.dma_start(xh_dram[c, :, :, bass.ds(g * P, P)], xh[:].bitcast(F32)).then_inc(tok_out, 16)
                sp.dma_start(xl_dram[c, :, :, bass.ds(g * P, P)], xl[:].bitcast(F32)).then_inc(tok_out, 16)

            for c in range(NC):
                last = c == NC - 1
                with sp.Fori(0, NG - 1 if last else NG) as g:
                    step(c, g, False)
                if last:
                    step(c, NG - 1, True)
            for g in range(TPC):
                T = NT - TPC + g
                sp.wait_ge(tok_out, 48 * T + 16)
                sp.dma_start(xt[:], x.rearrange("(t p) d -> t p d", p=P)[T]).then_inc(xt_in, 16)
                store_tile(T, NC - 1, g)

            sp.wait_ge(tok_out, 48 * NT + 16)
            sp.wait_ge(tok_tr2, NT)
            for u in range(2):
                sp.dma_start(w_raw[:, u, :], ffn_w[u]).then_inc(raw_in[u], 16)
            for c in range(NC):
                sp.dma_start(XH[c][:].bitcast(F32), xh_dram[c]).then_inc(XT_in[c], 16)
                sp.dma_start(XL[c][:].bitcast(F32), xl_dram[c]).then_inc(XT_in[c], 16)
            sp.dma_start(acc[:], x2_dram.rearrange("t p d -> p t d")).then_inc(acc_in, 16)
            with sp.Fori(1, UN // 2) as i:
                for s in range(2):
                    sp.wait_ge(w_hi_ok, 2 * i + s - 1)
                    sp.wait_ge(w_lo_ok, 2 * i + s - 1)
                    sp.sem_inc(held, 1)
                    sp.dma_start(w_raw[:, s, :], ffn_w[2 * i + s]).then_inc(raw_in[s], 16)
            ov = out.rearrange("(t p) d -> p t d", p=P)
            for c in range(NC):
                sp.wait_ge(y_used, TPC * NC * (GROUPS - 1) + TPC * (c + 1) + 4)
                sp.dma_start(ov[:, TPC * c:TPC * (c + 1), :], acc[:, TPC * c:TPC * (c + 1), :]).then_inc(out_done, 16)
            sp.wait_ge(out_done, 16 * NC)

        @block.gpsimd
        def _(pool):
            adj_v = adjT.rearrange("(j p) i -> p j i", p=P)

            def load_adj(c):
                for q in range(4):
                    pool.dma_start(adj[:, c % 2, 4 * q:4 * q + 4, :],
                                   adj_v[:, 4 * q:4 * q + 4, c * CH:(c + 1) * CH]).then_inc(adj_in[c % 2], 16)

            nc.gpsimd.memset(ident[:], 0.0).then_inc(su_pool, 1)
            nc.gpsimd.memset(ones[:], 1.0).then_inc(su_pool, 1)
            nc.gpsimd.memset(ones_bf[:], 1.0).then_inc(su_pool, 1)
            nc.gpsimd.memset(minus_half[:], -0.5).then_inc(su_pool, 1)
            pool.wait_ge(su_pool, 4)
            nc.gpsimd.affine_select(out=ident[:], in_=ident[:], compare_op=ALU.not_equal, fill=1.0, base=0,
                                    pattern=[[-1, P]], channel_multiplier=1).then_inc(const_ok, 1)
            for q in range(4):
                pool.wait_ge(su_dve, SU_VAR[q])
                nc.gpsimd.tensor_tensor(rs0[:, 1, 4 * q:4 * q + 4], rs0[:, 0, 4 * q:4 * q + 4],
                                        minus_half[:, 0:4], ALU.pow).then_inc(su_pool, 1)
                if q == 0:
                    load_adj(0)
                    load_adj(1)
            for c in range(NC):
                if c > 1:
                    pool.wait_ge(mask_ready, NB * H * (c - 1))
                    pool.wait_ge(av_ready, NG * NG * (c - 1))
                    load_adj(c)
                if c > 0:
                    with pool.Fori(0, TPC) as g:
                        T = TPC * (c - 1) + g
                        pool.wait_ge(tok_dve, S_ALL * T + S_VE)
                        nc.gpsimd.tensor_tensor(rs[:, 1:2], rs[:, 0:1], minus_half[:, 0:1], ALU.pow).then_inc(tok_rs, 1)
            with pool.Fori(NT - TPC, NT) as T:
                pool.wait_ge(tok_dve, S_ALL * T + S_VE)
                nc.gpsimd.tensor_tensor(rs[:, 1:2], rs[:, 0:1], minus_half[:, 0:1], ALU.pow).then_inc(tok_rs, 1)
            pool.wait_ge(tok_out, 48 * NT + 16)
            for e in range(E):
                nc.gpsimd.memset(rank[:, e:e + 1], float(E - e)).then_inc(const_ok, 1)

        @block.scalar
        def _(act):
            for t in range(NT):
                act.wait_ge(su_tr, t + 1)
                nc.scalar.copy(xT[:, :, t * P:(t + 1) * P],
                               bank[t % 2][:].rearrange("p (k i) -> p k i", k=KT)).then_inc(su_xT, 1)
                if t % TPC == TPC - 1:
                    c = t // TPC
                    act.wait_ge(su_sT, c + 1)
                    nc.scalar.copy(s21T[:, c * CH:(c + 1) * CH], bank[2 + c % 2][0:2 * H, :]).then_inc(su_sTc, 1)
            act.wait_ge(su_dve, SU_COLS[0])
            nc.scalar.activation(col_B[:], s2c[:], ACT.Exp).then_inc(su_act, 1)
            nc.scalar.activation(col_D[:], s2c[:], ACT.Exp, scale=0.2).then_inc(su_act, 1)
            nc.scalar.activation(row_a[:], ylo[:], ACT.Exp, scale=0.8).then_inc(su_act, 1)
            nc.scalar.activation(row_c[:], y_col[:], ACT.Exp, scale=-0.8).then_inc(su_act, 1)
            for t in range(NT):
                act.wait_ge(uvf_ready, t + 1)
                nc.scalar.copy(uv[:, t, :, 0:Q2], uvf[:, t % 2]).then_inc(hi_ready, 1)
                act.wait_ge(rest_ready, t + 1)
                nc.scalar.copy(uv[:, t, :, Q2:2 * Q2], uvf[:, t % 2]).then_inc(mid_ready, 1)

            act.wait_ge(uv_ready, NT)

            def relus(c, g, hh):
                it = NG * c + g
                act.wait_ge(s1_in[hh], 16 * (it + 1))
                for b in range(NB):
                    n = NB * (HB * it + hh) + b
                    act.wait_ge(batch_done, n + 1)
                    for k in range(ON_ACT[b]):
                        j = BJ * b + k
                        last = nc.scalar.activation(mask[:, b, k, :], s1_bc[:, hh, :], ACT.Relu, scale=BIG,
                                                    bias=s2_big[:, j, bass.ds(HB * g + hh, 1)])
                    last.then_inc(relu_ready, 1)

            def hidT_copy(T):
                act.wait_ge(tok_tr1, T + 2)
                nc.scalar.copy(hidT[:], TR[:].rearrange("p (k i) -> p k i", k=KT)).then_inc(tok_hidT, 1)

            def elu_exp(T):
                act.wait_ge(tok_dve, S_ALL * T + S_NEG)
                nc.scalar.activation(ez[:], ez[:], ACT.Exp).then_inc(tok_exp, 1)

            def xh_copy(T):
                act.wait_ge(tok_tr2, T + 1)
                act.wait_ge(tok_out, 48 * T + 16)
                nc.scalar.copy(xh[:], TR[:].rearrange("p (k i) -> p k i", k=KT)).then_inc(tok_xh, 1)

            for c in range(NC):
                with act.Fori(0, NG) as g:
                    T = NG * (c - 1) + g
                    relus(c, g, 0)
                    if c > 0:
                        hidT_copy(T)
                    relus(c, g, 1)
                    relus(c, g, 2)
                    if c > 0:
                        elu_exp(T)
                    relus(c, g, 3)
                    if c > 0:
                        xh_copy(T)
            for T in range(NT - TPC, NT):
                hidT_copy(T)
                elu_exp(T)
                xh_copy(T)

            def split_hi(grp, s, par):
                act.wait_ge(raw_in[s], 16 * (grp + 1))
                if not isinstance(grp, int) or grp > 0:
                    act.wait_ge(y_ready, TPC * NC * (grp - 1) + 2 * TPC)
                nc.scalar.copy(w_hi[:, par, s, :], w_raw[:, s, :]).then_inc(w_hi_ok, 1)

            def silu(S):
                for ht in range(GH):
                    n = GH * S + ht
                    act.wait_ge(h1_ready, n + 1)
                    act.wait_ge(g_ready, n + 1)
                    nc.scalar.activation(act_s[:, ht, :], bank[2 * ht][:], ACT.Silu).then_inc(silu_ready, 1)

            split_hi(0, 0, 0)
            split_hi(0, 1, 0)
            act.wait_ge(gate_dve, GATE_EXP)
            nc.scalar.activation(top[:, 2, :], top[:, 2, :], ACT.Exp).then_inc(gate_exp, 1)
            silu(0)

            def two_groups(i, last):
                for k in range(2 * NC):
                    grp = 2 * i + k // NC
                    S = 2 * NC * i + k
                    if not (last and k == 2 * NC - 1):
                        silu(S + 1)
                    if k % NC < GH and not (last and k >= NC):
                        split_hi(grp + 1, k % NC, (k // NC + 1) % 2)

            with act.Fori(0, GROUPS // 2 - 1) as i:
                two_groups(i, False)
            two_groups(GROUPS // 2 - 1, True)

        @block.tensor
        def _(pe):
            mm = nc.tensor.matmul
            pe.sem_inc(batch_done, NB)
            pe.sem_inc(sums_free, 2)
            pe.sem_inc(av_free, 2)
            pe.sem_inc(tok_tr1, 1)
            pe.sem_inc(g_ready, GH)
            pe.sem_inc(y_ready, 2 * TPC)
            pe.sem_inc(y_used, TPC)

            pe.wait_ge(const_ok, 1)
            for t in range(NT):
                pe.wait_ge(su_dve, SU_XN[t])
                if t >= 2:
                    pe.wait_ge(su_xT, t - 1)
                for k in range(KT):
                    last = nc.tensor.transpose(bank[t % 2][:, k * P:(k + 1) * P], xall[:, t, k * P:(k + 1) * P], ident[:])
                last.then_inc(su_tr, 1)
                if t % TPC == TPC - 1:
                    c = t // TPC
                    pe.wait_ge(su_xT, t + 1)
                    if c >= 2:
                        pe.wait_ge(su_sTc, c - 1)
                    for k in range(KT):
                        last = mm(bank[2 + c % 2][0:2 * H, :], w12[:, k, :], xT[:, k, c * CH:(c + 1) * CH],
                                  start=(k == 0), stop=(k == KT - 1))
                    last.then_inc(su_sT, 1)
            pe.wait_ge(su_dve, SU_DIAG[0])
            mm(bank[1][:, 0:H], ones[0:H, :], gdiag[:], start=True, stop=True).then_inc(su_g, 1)
            for t in range(NT):
                for k in range(KT):
                    last = mm(bank[0][:, t * 2 * H:(t + 1) * 2 * H], xT[:, k, t * P:(t + 1) * P], w12[:, k, :],
                              start=(k == 0), stop=(k == KT - 1))
            last.then_inc(su_cols, 1)
            for t in range(NT):
                if t >= 2:
                    pe.wait_ge(seq_used, t - 1)
                else:
                    pe.wait_ge(su_sTc, NC)
                for k in range(KT):
                    last = mm(bank[2 + t % 2][:], xT[:, k, t * P:(t + 1) * P], w_seq[:, k, :],
                              start=(k == 0), stop=(k == KT - 1))
                last.then_inc(seq_ready, 1)

            def degrees(c):
                pe.wait_ge(adj_in[c % 2], 64 * (c // 2 + 1))
                if c >= 2:
                    pe.wait_ge(tok_dve, S_ALL * TPC * (c - 1))
                for j in range(NT):
                    last = mm(bank[DEG_BANK][:], ones_bf[:], adj[:, c % 2, j, :], start=(j == 0), stop=(j == NT - 1))
                last.then_inc(deg_ready, 1)

            def head(c, g, hh):
                it = NG * c + g
                pe.wait_ge(sums_free, HB * it + hh + 1)
                for b in range(NB):
                    pe.wait_ge(mask_ready, NB * (HB * it + hh) + b + 1)
                    for k in range(BJ):
                        j = BJ * b + k
                        rhs = uv[:, j, bass.ds(HB * g + hh, 1), :].rearrange("p o q -> p (o q)")
                        for t in range(TPC):
                            o = (t % 2) * PARTS * Q2
                            last = mm(bank[2 * (hh % 2) + t // 2][:, o:o + PARTS * Q2], mask[:, b, k, t * P:(t + 1) * P],
                                      rhs, start=(j == 0 and t % 2 == 0), stop=(j == NT - 1), skip_group_check=True)
                    last.then_inc(batch_done, 1)

            def adj_v(c, g, qs):
                it = NG * c + g
                for q in qs:
                    pe.wait_ge(av_free, NG * it + q + 1)
                    for j in range(NT):
                        rhs = uv[:, j, HB * q:HB * (q + 1), :].rearrange("p h (r q) -> p h r q", r=PARTS)[:, :, :, Q:Q2]
                        last = mm(bank[4 + q % 2][:, 0:HB * PARTS * Q], adj[:, c % 2, j, bass.ds(g * P, P)], rhs,
                                  start=(j == 0), stop=(j == NT - 1))
                    last.then_inc(av_ready, 1)

            def tok_transpose(T):
                pe.wait_ge(tok_dve, S_ALL * T + S_HID)
                for k in range(KT):
                    last = nc.tensor.transpose(TR[:, k * P:(k + 1) * P], hid[:, k * P:(k + 1) * P], ident[:])
                last.then_inc(tok_tr1, 1)

            def tok_project(T):
                pe.wait_ge(tok_hidT, T + 1)
                for k in range(KT):
                    last = mm(PR[:], hidT[:, k, :], w_out[:, k, :], start=(k == 0), stop=(k == KT - 1))
                last.then_inc(tok_proj, 1)

            def tok_transpose2(T):
                pe.wait_ge(tok_dve, S_ALL * T + S_XN)
                for k in range(KT):
                    last = nc.tensor.transpose(TR[:, k * P:(k + 1) * P], xn[:, k * P:(k + 1) * P], ident[:])
                last.then_inc(tok_tr2, 1)

            pe.wait_ge(uv_ready, NT)
            pe.wait_ge(wo_in, 32)
            for c in range(NC):
                degrees(c)
                pe.wait_ge(adj_ok, 4 * (c + 1))
                with pe.Fori(0, NG) as g:
                    T = NG * (c - 1) + g
                    if c > 0:
                        tok_transpose(T)
                    head(c, g, 0)
                    adj_v(c, g, (0, 1))
                    if c > 0:
                        tok_project(T)
                    head(c, g, 1)
                    head(c, g, 2)
                    adj_v(c, g, (2, 3))
                    head(c, g, 3)
                    if c > 0:
                        tok_transpose2(T)
            for T in range(NT - TPC, NT):
                tok_transpose(T)
                tok_project(T)
                tok_transpose2(T)

            def three(out_, hi, lo, rhi, rlo, start, stop):
                mm(out_, hi, rhi, start=start, stop=False)
                mm(out_, hi, rlo, start=False, stop=False)
                return mm(out_, lo, rhi, start=False, stop=stop)

            def up(S, grp, par, c):
                if c == 0:
                    pe.wait_ge(w_hi_ok, GH * (grp + 1))
                    pe.wait_ge(w_lo_ok, GH * (grp + 1))
                pe.wait_ge(XT_in[c], 32)
                for ht in range(GH):
                    pe.wait_ge(g_ready, GH * S + ht + 1)
                    for s, done in ((0, h1_ready), (1, h2_ready)):
                        for k in range(KT):
                            o = s * D + k * P
                            last = three(bank[2 * ht + s][:], w_hi[:, par, ht, o:o + P], w_lo[:, par, ht, o:o + P],
                                         XH[c][:, k, :], XL[c][:, k, :], k == 0, k == KT - 1)
                        last.then_inc(done, 1)

            def down(S, grp, par, hpar, c):
                pe.wait_ge(hid_ready, GH * (S + 1))
                for tt in range(TPC):
                    pe.wait_ge(y_used, TPC * S + tt + 1)
                    for ht in range(GH):
                        last = three(bank[4 + tt][:], h_hi[:, hpar, ht, tt * P:(tt + 1) * P],
                                     h_lo[:, hpar, ht, tt * P:(tt + 1) * P],
                                     w_hi[:, par, ht, 2 * D:], w_lo[:, par, ht, 2 * D:], ht == 0, ht == GH - 1)
                    last.then_inc(y_ready, 1)

            up(0, 0, 0, 0)
            pe.wait_ge(tok_dve, S_ALL * NT)
            for t in range(NT):
                c, o = t // TPC, (t % TPC) * P
                if o == 0:
                    pe.wait_ge(XT_in[c], 32)
                for k in range(KT):
                    last = three(bank[4][:, t * E:(t + 1) * E], XH[c][:, k, o:o + P], XL[c][:, k, o:o + P],
                                 wg_hi[:, k, :], wg_lo[:, k, :], k == 0, k == KT - 1)
            last.then_inc(sc_ready, 1)
            pe.wait_ge(gate_dve, 1)

            def two_groups(i, last):
                for k in range(2 * NC):
                    grp = 2 * i + k // NC
                    S = 2 * NC * i + k
                    if not (last and k == 2 * NC - 1):
                        k1 = k + 1
                        up(S + 1, 2 * i + k1 // NC, (k1 // NC) % 2, k1 % NC)
                    down(S, grp, (k // NC) % 2, k % 2, k % NC)

            with pe.Fori(0, GROUPS // 2 - 1) as i:
                two_groups(i, False)
            two_groups(GROUPS // 2 - 1, True)


def kernel(**inputs):
    import numpy as np
    import concourse.bacc as bacc
    from concourse.bass_utils import run_bass_kernel_spmd

    a = {k: np.asarray(v) for k, v in inputs.items()}

    def up_layout(w):
        return w.reshape(E, HID // P, P, KT, P).transpose(0, 1, 4, 3, 2).reshape(UN, P, D)

    w3 = a["L0_ffn_W3"].reshape(E, D, HID // P, P).transpose(0, 2, 3, 1).reshape(UN, P, D)
    arrays = {
        "x": a["x"], "adjT": a["adj"].T, "W_seq": a["L0_gnn_W_seq"], "a1": a["L0_gnn_a1"], "a2": a["L0_gnn_a2"],
        "W_out": a["L0_gnn_W_out"], "b_out": a["L0_gnn_b_out"], "WgT": a["L0_ffn_Wg"].T,
        "ffn_w": np.concatenate([up_layout(a["L0_ffn_W1"]), up_layout(a["L0_ffn_W2"]), w3], axis=2),
    }
    arrays = {k: np.ascontiguousarray(v) for k, v in arrays.items()}
    nc = bacc.Bacc("TRN2", target_bir_lowering=False, num_devices=1, dynamic_dma_scratch_size=4096)
    args = [nc.dram_tensor(k, v.shape, mybir.dt.from_np(v.dtype), kind="ExternalInput").ap() for k, v in arrays.items()]
    args.append(nc.dram_tensor("out", (N, D), F32, kind="ExternalOutput").ap())
    build(nc, *args)
    r = run_bass_kernel_spmd(nc, [arrays], core_ids=[0])
    return r.results[0]["out"]
```

```python
import concourse.bass as bass
from concourse import mybir
from contextlib import ExitStack

F32 = mybir.dt.float32
F32R = mybir.dt.float32r
F8 = mybir.dt.float8e5
U8 = mybir.dt.uint8
BF16 = mybir.dt.bfloat16
I32 = mybir.dt.int32
ALU = mybir.AluOpType
ACT = mybir.ActivationFunctionType
AX = mybir.AxisListType

P = 128
N, D = 2048, 512
H, DH = 16, 32
E, HID = 8, 1024
KT = D // P
NT = N // P
CH = 512
NC = N // CH
TPC = CH // P
Q = DH + 1
Q2 = 2 * Q
PARTS = 3
EPS = 1e-5
BIG = float(2 ** 60)

HG = 4
NG = H // HG
BJ = 4
NB = NT // BJ
SLOTS = NB * H
RING = 8
ON_ACT = 3
ONE8 = 0x3C
AVS = 5

TILE_BYTES = 6 * D * 4
SEQ_REST = (NT - TPC - KT - 1) * D * 4 - TILE_BYTES
SETUP_AT = (TILE_BYTES + SEQ_REST + NT * HG * Q2 * 4 + 2 * NT * H * 4 + 2 * NT * CH
            + NT * H * PARTS * Q2 * 2 + 4 * NT * H * 4)
UN = E * HID // P
GH = 2
GPE = HID // P // GH
GROUPS = UN // GH
WU = 2 * KT * P + D


def build(nc, x, adjT, W_seq, a1, a2, W_out, b_out, WgT, ffn_w, out):
    ctx = ExitStack()
    with ctx:
        def keep(name, shape, dt, where=None):
            return (where or ctx).enter_context(nc.sbuf_tensor(name, shape, dt))

        def sem(name):
            return ctx.enter_context(nc.semaphore(name))

        s1_rows = nc.dram_tensor("s1_rows", [NC * H, CH], F32, kind="Internal").ap()
        x2_dram = nc.dram_tensor("x2_dram", [NT - TPC, P, D], F32, kind="Internal").ap()
        xh_dram = nc.dram_tensor("xh_dram", [NC - 1, P, KT, CH], F32, kind="Internal").ap()
        xl_dram = nc.dram_tensor("xl_dram", [NC - 1, P, KT, CH], F32, kind="Internal").ap()

        ident = keep("ident", [P, P], F32)
        ones = keep("ones", [P, P], F32)
        ones_bf = keep("ones_bf", [P, P], BF16)
        wg = keep("wg", [P, KT, E], F32)
        wg_hi = keep("wg_hi", [P, KT, E], F32R)
        wg_lo = keep("wg_lo", [P, KT, E], F32R)
        gates = keep("gates", [P, NT, E], F32)
        minus_half = keep("minus_half", [P, TPC], F32)

        bank = [ctx.enter_context(nc.psum_tensor(f"bank{i}", [P, 512], F32)) for i in range(8)]

        bst = keep("bst", [P, 6], F32)
        mv = keep("mv", [P, 2], F32)
        rs = keep("rs", [P, 4], F32)
        bst4 = keep("bst4", [P, TPC, 6], F32)
        mv4 = keep("mv4", [P, TPC, 2], F32)
        rs4 = keep("rs4", [P, 4, TPC], F32)
        hid = keep("hid", [P, TPC, D], F32)
        X1 = ExitStack()
        seq = keep("seq", [P, NT, D], F32, X1)
        X1.close()
        hidT = keep("hidT", [P, TPC, KT, P], F32)
        w_out = keep("w_out", [P, KT, D], F32)
        b_row = keep("b_row", [P, D], F32)
        A = ExitStack()
        z = keep("z", [P, D], F32, A)
        ez = keep("ez", [P, D], F32, A)
        xt = keep("xt", [P, D], F32, A)
        xn = keep("xn", [P, D], F32, A)
        xh = keep("xh", [P, KT, P], F32R, A)
        xl = keep("xl", [P, KT, P], F32R, A)
        keep("rest_of_seq", [P, SEQ_REST], U8, A)
        uvf = keep("uvf", [P, NT, HG, Q2], F32, A)
        col_B = keep("col_B", [P, NT, H], F32, A)
        col_D = keep("col_D", [P, NT, H], F32, A)
        adj = keep("adj", [P, NT, CH], F8, A)
        adj_next = keep("adj_next", [P, NT, CH], F8, A)
        X0 = ExitStack()
        xall = keep("xall", [P, NT, D], F32, X0)
        wtmp = keep("wtmp", [P, KT * H, DH], F32, X0)
        a_rows = keep("a_rows", [P, 2, DH], F32, X0)
        xT = keep("xT", [P, KT, N], F32, X0)
        w_seq = keep("w_seq", [P, KT, D], F32, X0)
        X0.close()
        uv = keep("uv", [P, NT, H, PARTS * Q2], BF16, A)
        s2_big = keep("s2_big", [P, NT, H], F32, A)
        s2_neg = keep("s2_neg", [P, NT, H], F32, A)
        row_a = keep("row_a", [P, NT, H], F32, A)
        row_c = keep("row_c", [P, NT, H], F32, A)
        s1_bc = keep("s1_bc", [P, HG, CH], F32, A)
        mask = keep("mask", [P, RING, BJ, CH], F8, A)
        sums = keep("sums", [P, TPC, HG, Q2], F32, A)
        av = keep("av", [P, 2, TPC, HG, Q], F32, A)
        rden = keep("rden", [P, TPC, HG], F32, A)
        empty = keep("empty", [P, CH], U8, A)
        A.close()
        X2 = ExitStack()
        keep("below", [P, SETUP_AT], U8, X2)
        w12 = keep("w12", [P, KT, 2 * H], F32, X2)
        s21T = keep("s21T", [2 * H, N], F32, X2)
        gmax = keep("gmax", [H, 1], F32, X2)
        gdiag = keep("gdiag", [H, H], F32, X2)
        gcol = keep("gcol", [P, H], F32, X2)
        y_col = keep("y_col", [P, NT, H], F32, X2)
        ylo = keep("ylo", [P, NT, H], F32, X2)
        s2c = keep("s2c", [P, NT, H], F32, X2)
        bst0 = keep("bst0", [P, NT, 6], F32, X2)
        mv0 = keep("mv0", [P, NT, 2], F32, X2)
        rs0 = keep("rs0", [P, 4, NT], F32, X2)
        X2.close()

        B = ctx
        w_raw = keep("w_raw", [P, 2, WU], F32, B)
        w_hi, w_lo = [keep("w_hi0", [P, GH, WU], F32R, B)], [keep("w_lo0", [P, GH, WU], F32R, B)]
        X3 = ExitStack()
        z4 = keep("z4", [P, TPC, D], F32, X3)
        ez4 = keep("ez4", [P, TPC, D], F32, X3)
        xn4 = keep("xn4", [P, TPC, D], F32, X3)
        X3.close()
        w_hi.append(keep("w_hi1", [P, GH, WU], F32R, B))
        w_lo.append(keep("w_lo1", [P, GH, WU], F32R, B))
        h_hi = keep("h_hi", [P, 2, GH, CH], F32R, B)
        h_lo = keep("h_lo", [P, 2, GH, CH], F32R, B)
        act_s = keep("act_s", [P, GH, CH], F32, B)
        act_g = keep("act_g", [P, GH, CH], F32, B)
        XH = [keep(f"XH{c}", [P, KT, CH], F32R, B) for c in range(NC)]
        XL = [keep(f"XL{c}", [P, KT, CH], F32R, B) for c in range(NC)]
        acc = keep("acc", [P, NT, D], F32, B)
        scT = keep("scT", [E, N], F32, B)
        sc = keep("sc", [P, NT, E], F32, B)
        eq1 = keep("eq1", [P, NT, E], F32, B)
        eq2 = keep("eq2", [P, NT, E], F32, B)
        rank = keep("rank", [P, E], F32, B)
        top = keep("top", [P, 6, NT], F32, B)

        x_in = [sem(f"x_in{i}") for i in range(4)]
        w_in = sem("w_in")
        wo_in = sem("wo_in")
        s1_out = sem("s1_out")
        adj_in = sem("adj_in")
        s1_in = [sem(f"s1_in{i}") for i in range(HG)]
        xt_in = sem("xt_in")
        x2_out = sem("x2_out")
        xhl_out = sem("xhl_out")
        raw_in = [sem(f"raw_in{i}") for i in range(2)]
        XT_in = [sem(f"XT_in{c}") for c in range(NC - 1)]
        acc_in = sem("acc_in")
        last_in = sem("last_in")
        out_done = sem("out_done")
        const_ok = sem("const_ok")
        su_dve = sem("su_dve")
        su_act = sem("su_act")
        su_pool = sem("su_pool")
        su_tr = sem("su_tr")
        su_xT = sem("su_xT")
        su_sT = sem("su_sT")
        su_sTc = sem("su_sTc")
        su_cols = sem("su_cols")
        su_g = sem("su_g")
        seq_ready = sem("seq_ready")
        seq_kept = sem("seq_kept")
        uvf_ready = sem("uvf_ready")
        hi_ready = sem("hi_ready")
        rest_ready = sem("rest_ready")
        mid_ready = sem("mid_ready")
        uv_ready = sem("uv_ready")
        held = sem("held")
        relu_ready = sem("relu_ready")
        mask_ready = sem("mask_ready")
        batch_done = sem("batch_done")
        sums_free = sem("sums_free")
        av_ready = sem("av_ready")
        av_free = sem("av_free")
        deg_ready = sem("deg_ready")
        empty_ready = sem("empty_ready")
        adj_ok = sem("adj_ok")
        comb = sem("comb")
        tok_tr1 = sem("tok_tr1")
        tok_hidT = sem("tok_hidT")
        tok_proj = sem("tok_proj")
        tok_z = sem("tok_z")
        tok_exp = sem("tok_exp")
        tok_x = sem("tok_x")
        tok_rs = sem("tok_rs")
        tok_n = sem("tok_n")
        tok_tr2 = sem("tok_tr2")
        tok_xh = sem("tok_xh")
        tok_low = sem("tok_low")
        last_tr1 = sem("last_tr1")
        last_hidT = sem("last_hidT")
        last_proj = sem("last_proj")
        last_z = sem("last_z")
        last_exp = sem("last_exp")
        last_x = sem("last_x")
        last_rs = sem("last_rs")
        last_n = sem("last_n")
        last_tr2 = sem("last_tr2")
        last_xh = sem("last_xh")
        last_low = sem("last_low")
        w_hi_ok = sem("w_hi_ok")
        w_lo_ok = sem("w_lo_ok")
        h1_ready = sem("h1_ready")
        h2_ready = sem("h2_ready")
        silu_ready = sem("silu_ready")
        g_ready = sem("g_ready")
        hi_done = sem("hi_done")
        hid_ready = sem("hid_ready")
        y_ready = sem("y_ready")
        y_used = sem("y_used")
        row_ready = sem("row_ready")
        row_kept = sem("row_kept")
        sc_ready = sem("sc_ready")
        gate_dve = sem("gate_dve")
        gate_exp = sem("gate_exp")

        Z_ALL, X_ALL, N_ALL, C_ALL = 2, 5, 4, 6
        TR, PR = bank[6], bank[7]
        C_LAST, T_LAST = NC - 1, NT - TPC
        HIDDEN_DONE = C_ALL * NG * NC
        LAST_VAR = 4 * TPC + 1
        V32 = lambda ap: ap.bitcast(I32)

        TAKE = {NB * h + NB - 1 + 6: h for h in range(H)}
        AV_DONE = [-(-NT * (p + 1) // AVS) - 1 for p in range(NT)]
        TAKE_AV = {t + 6: p for p, t in enumerate(AV_DONE)}
        COMBINE = {NB * HG * (g + 1) - 1 + 7: g for g in range(NG)}
        TR1 = {8: 0, 9: 1, 16: 2, 17: 3}
        HIDT = {14: 0, 15: 1, 22: 2, 23: 3}
        PROJ = {24 + 8 * k: k for k in range(TPC)}
        TOK_Z = {30 + 8 * k: k for k in range(TPC)}
        TOK_EXP = {31 + 8 * k: k for k in range(TPC)}
        TOK_X = {32 + 8 * k: k for k in range(TPC)}
        TOK_N = {34 + 8 * k: k for k in range(TPC)}
        TR2 = {35 + 8 * k: k for k in range(TPC)}
        TOK_HL = {min(41 + 8 * k, SLOTS - 1): k for k in range(TPC)}
        DEGREES = 58

        block = ctx.enter_context(nc.Block())

        SU_VAR, SU_XN, SU_DIAG, SU_COLS, SU_W12 = [0] * 4, [0] * NT, [0], [0], [0]
        GATE_EXP = 13

        SU = [0]

        def setup_vector(dve):
            def step(ins, wait=None):
                ins.then_inc(su_dve, 1)
                SU[0] += 1
                return SU[0]

            def settle():
                dve.wait_ge(su_dve, SU[0])

            for q in range(4):
                dve.wait_ge(x_in[q], 16)
                ts = range(4 * q, 4 * q + 4)
                for t in ts:
                    step(nc.vector.bn_stats(bst0[:, t, :], xall[:, t, :]))
                settle()
                for t in ts:
                    step(nc.vector.bn_aggr(mv0[:, t, :], bst0[:, t, :]))
                settle()
                qs = slice(4 * q, 4 * q + 4)
                SU_VAR[q] = step(nc.vector.tensor_scalar(rs0[:, 0, qs], mv0[:, qs, 1], EPS, None, ALU.add))
                dve.wait_ge(su_pool, 5 + q)
                newton(dve, rs0[:, 0, qs], rs0[:, 1, qs], rs0[:, 2, qs], step, settle)
                settle()
                for t in ts:
                    SU_XN[t] = step(nc.vector.tensor_scalar(xall[:, t, :], xall[:, t, :], mv0[:, t, 0:1],
                                                            rs0[:, 1, t:t + 1], ALU.subtract, ALU.mult))
                if q == 0:
                    score_weights(dve, step, settle)
            dve.wait_ge(su_sTc, NC)
            step(nc.vector.reduce_max(gmax[:], s21T[0:H, :], axis=AX.X))
            settle()
            SU_DIAG[0] = step(nc.vector.tensor_scalar(gdiag[:], ident[0:H, 0:H], gmax[:, 0:1], None, ALU.mult))
            dve.wait_ge(su_g, 1)
            step(nc.vector.tensor_copy(gcol[:], bank[1][:, 0:H]))
            settle()
            gb = gcol[:].unsqueeze(1).broadcast_to([P, NT, H])
            cols = bank[0][:].rearrange("p (t s) -> p t s", t=NT)
            dve.wait_ge(su_cols, 1)
            step(nc.vector.tensor_tensor(s2c[:], cols[:, :, 0:H], gb, ALU.subtract))
            step(nc.vector.tensor_tensor(y_col[:], cols[:, :, H:2 * H], gb, ALU.add))
            step(nc.vector.tensor_scalar(s2_big[:], cols[:, :, 0:H], BIG, None, ALU.mult))
            step(nc.vector.tensor_scalar(s2_neg[:], cols[:, :, 0:H], -1.0, None, ALU.mult))
            settle()
            step(nc.vector.tensor_scalar(ylo[:], y_col[:], 0.0, None, ALU.min))
            settle()
            SU_COLS[0] = step(nc.vector.tensor_scalar(y_col[:], y_col[:], 0.0, None, ALU.max))

        def score_weights(dve, step, settle):
            dve.wait_ge(w_in, 64)
            wv = w_seq[:].rearrange("p k (h d) -> p (k h) d", d=DH)
            for s in range(2):
                settle()
                step(nc.vector.tensor_tensor(wtmp[:], wv, a_rows[:, 1 - s, :].unsqueeze(1).broadcast_to([P, KT * H, DH]),
                                             ALU.mult))
                settle()
                step(nc.vector.tensor_reduce(w12[:, :, s * H:(s + 1) * H],
                                             wtmp[:].rearrange("p (k h) d -> p k h d", k=KT),
                                             axis=AX.X, op=ALU.add))
            step(nc.vector.tensor_copy(wg_hi[:], wg[:]))
            settle()
            step(nc.vector.tensor_tensor(wg_lo[:], wg[:], wg_hi[:].bitcast(F32), ALU.subtract))
            SU_W12[0] = SU[0]

        def newton(dve, v, y, t, step, settle):
            step(nc.vector.tensor_tensor(t, y, y, ALU.mult))
            settle()
            step(nc.vector.tensor_tensor(t, t, v, ALU.mult))
            settle()
            step(nc.vector.tensor_scalar(t, t, -0.5, 1.5, ALU.mult, ALU.add))
            settle()
            step(nc.vector.tensor_tensor(y, y, t, ALU.mult))

        @block.vector
        def _(dve):
            dve.wait_ge(const_ok, 1)
            setup_vector(dve)
            TH = NT // 2

            def uv_make(g, half):
                n = 2 * g + half
                ts, hs = slice(TH * half, TH * (half + 1)), slice(HG * g, HG * (g + 1))
                if n == 0:
                    dve.wait_ge(su_act, 4)
                    dve.wait_ge(seq_kept, NT)
                if g > 0:
                    dve.wait_ge(uv_ready, n - 1)
                u = uvf[:, ts]
                sv = seq[:, ts, D // NG * g:D // NG * (g + 1)].rearrange("p t (h d) -> p t h d", d=DH)
                for s, f in ((0, col_B), (1, col_D)):
                    nc.vector.tensor_tensor(u[:, :, :, s * Q:s * Q + DH], sv,
                                            f[:, ts, hs].unsqueeze(3).broadcast_to([P, TH, HG, DH]), ALU.mult)
                    last = nc.vector.tensor_copy(u[:, :, :, s * Q + DH], f[:, ts, hs])
                last.then_inc(uvf_ready, 1)

            def uv_rest(g, half, low):
                n = 2 * g + half
                ts, hs = slice(TH * half, TH * (half + 1)), slice(HG * g, HG * (g + 1))
                part = uv[:, ts, hs, :]
                k = 1 if low else 0
                dve.wait_ge(mid_ready if low else hi_ready, n + 1)
                out_ = part[:, :, :, 2 * Q2:] if low else uvf[:, ts]
                nc.vector.tensor_tensor(out_, uvf[:, ts], part[:, :, :, k * Q2:(k + 1) * Q2],
                                        ALU.subtract).then_inc(uv_ready if low else rest_ready, 1)

            def fix_adj(c):
                dve.wait_ge(deg_ready, c + 1)
                nc.vector.tensor_scalar(empty[:], PR[:], 0.0, float(ONE8), ALU.is_equal, ALU.mult).then_inc(empty_ready, 1)
                if not isinstance(c, int):
                    dve.wait_ge(av_ready, NT * c)
                dve.wait_ge(empty_ready, c + 1)
                for q in range(4):
                    js = slice(4 * q, 4 * q + 4)
                    nc.vector.tensor_tensor(V32(adj[:, js, :]), V32(adj_next[:, js, :]),
                                            V32(empty[:]).unsqueeze(1).broadcast_to([P, 4, CH // 4]),
                                            ALU.bitwise_or).then_inc(adj_ok, 1)
                dve.wait_ge(adj_ok, 4 * (c + 1))

            def masks(c, n):
                h, b = n // NB, n % NB
                dve.wait_ge(relu_ready, SLOTS * c + n + 1)
                m = V32(mask[:, n % RING, 0:ON_ACT, :])
                last = nc.vector.tensor_tensor(m, m, V32(adj[:, BJ * b:BJ * b + ON_ACT, :]), ALU.bitwise_and)
                for k in range(ON_ACT, BJ):
                    j = BJ * b + k
                    last = nc.vector.scalar_tensor_tensor(mask[:, n % RING, k, :].bitcast(U8), s1_bc[:, h % HG, :],
                                                          s2_neg[:, j, h:h + 1], adj[:, j, :].bitcast(U8),
                                                          ALU.is_gt, ALU.mult)
                last.then_inc(mask_ready, 1)

            def take_sums(c, h):
                dve.wait_ge(batch_done, NB * (H * c + h + 1) + RING)
                for q in range(2):
                    last = nc.vector.tensor_reduce(
                        sums[:, 2 * q:2 * q + 2, h % HG, :],
                        bank[2 * (h % 2) + q][:, 0:2 * PARTS * Q2].rearrange("p (t r q) -> p t q r", t=2, r=PARTS),
                        axis=AX.X, op=ALU.add)
                last.then_inc(sums_free, 1)

            def take_av(c, p):
                g, t = p // TPC, p % TPC
                dve.wait_ge(av_ready, NT * c + p + 1)
                nc.vector.tensor_reduce(
                    av[:, g % 2, t],
                    bank[4 + p % 2][:, 0:HG * PARTS * Q].rearrange("p (h r q) -> p h q r", h=HG, r=PARTS),
                    axis=AX.X, op=ALU.add).then_inc(av_free, 1)

            def combine(c, g):
                n = C_ALL * (NG * c + g)
                a, u, v = av[:, g % 2], sums[:, :, :, 0:Q], sums[:, :, :, Q:Q2]
                ra, rc = (f[:, bass.ds(TPC * c, TPC), HG * g:HG * (g + 1)].unsqueeze(3).broadcast_to([P, TPC, HG, Q])
                          for f in (row_a, row_c))
                dve.wait_ge(sums_free, HG * (NG * c + g + 1) + 2)
                dve.sem_inc(held, 1)
                nc.vector.tensor_tensor(a, a, v, ALU.subtract).then_inc(comb, 1)
                nc.vector.tensor_tensor(u, u, ra, ALU.mult).then_inc(comb, 1)
                dve.wait_ge(comb, n + 1)
                nc.vector.tensor_tensor(a, a, rc, ALU.mult).then_inc(comb, 1)
                dve.wait_ge(comb, n + 3)
                nc.vector.tensor_tensor(a, a, u, ALU.add).then_inc(comb, 1)
                dve.wait_ge(comb, n + 4)
                nc.vector.reciprocal(rden[:], a[:, :, :, DH]).then_inc(comb, 1)
                dve.wait_ge(comb, n + 5)
                dve.wait_ge(tok_tr1, TPC * c + 1)
                nc.vector.tensor_tensor(hid[:, :, D // NG * g:D // NG * (g + 1)].rearrange("p t (h d) -> p t h d", d=DH),
                                        a[:, :, :, 0:DH], rden[:].unsqueeze(3).broadcast_to([P, TPC, HG, DH]),
                                        ALU.mult).then_inc(comb, 1)

            def token_z(T):
                dve.wait_ge(tok_proj, T + 1)
                nc.vector.tensor_tensor(z[:], PR[:], b_row[:], ALU.add).then_inc(tok_z, 1)
                dve.wait_ge(tok_z, Z_ALL * T + 1)
                nc.vector.tensor_scalar(ez[:], z[:], 0.0, None, ALU.min).then_inc(tok_z, 1)

            def token_x(T):
                n = X_ALL * T
                dve.wait_ge(tok_exp, T + 1)
                nc.vector.scalar_tensor_tensor(ez[:], z[:], 0.0, ez[:], ALU.max, ALU.add).then_inc(tok_x, 1)
                dve.wait_ge(tok_x, n + 1)
                dve.wait_ge(xt_in, 16 * (T + 1))
                nc.vector.scalar_tensor_tensor(xt[:], ez[:], -1.0, xt[:], ALU.add, ALU.add).then_inc(tok_x, 1)
                dve.wait_ge(tok_x, n + 2)
                nc.vector.bn_stats(bst[:], xt[:]).then_inc(tok_x, 1)
                dve.wait_ge(tok_x, n + 3)
                dve.sem_inc(held, 1)
                nc.vector.bn_aggr(mv[:], bst[:]).then_inc(tok_x, 1)
                dve.wait_ge(tok_x, n + 4)
                nc.vector.tensor_scalar(rs[:, 0:1], mv[:, 1:2], EPS, None, ALU.add).then_inc(tok_x, 1)

            def token_norm(T):
                n = N_ALL * T
                dve.wait_ge(tok_rs, T + 1)
                nc.vector.scalar_tensor_tensor(rs[:, 2:3], rs[:, 1:2], rs[:, 1:2], rs[:, 0:1],
                                               ALU.mult, ALU.mult).then_inc(tok_n, 1)
                dve.wait_ge(tok_n, n + 1)
                nc.vector.tensor_scalar(rs[:, 2:3], rs[:, 2:3], -0.5, 1.5, ALU.mult, ALU.add).then_inc(tok_n, 1)
                dve.wait_ge(tok_n, n + 2)
                nc.vector.tensor_tensor(rs[:, 3:4], rs[:, 1:2], rs[:, 2:3], ALU.mult).then_inc(tok_n, 1)
                dve.wait_ge(tok_n, n + 3)
                nc.vector.tensor_scalar(xn[:], xt[:], mv[:, 0:1], rs[:, 3:4], ALU.subtract, ALU.mult).then_inc(tok_n, 1)

            def token_low(T):
                dve.wait_ge(tok_xh, T + 1)
                nc.vector.tensor_tensor(xl[:], TR[:].rearrange("p (k i) -> p k i", k=KT), xh[:].bitcast(F32),
                                        ALU.subtract).then_inc(tok_low, 1)

            def chunk(c):
                first = isinstance(c, int)
                T = TPC * (c - 1)
                fix_adj(c)
                for n in range(SLOTS):
                    masks(c, n)
                    if n + SLOTS in TAKE and not first:
                        take_sums(c - 1, TAKE[n + SLOTS])
                    if n in TAKE:
                        take_sums(c, TAKE[n])
                    if n in TAKE_AV:
                        take_av(c, TAKE_AV[n])
                    if n + SLOTS in COMBINE and not first:
                        combine(c - 1, COMBINE[n + SLOTS])
                    if n in COMBINE:
                        combine(c, COMBINE[n])
                    if not first:
                        if n in TOK_Z:
                            token_z(T + TOK_Z[n])
                        if n in TOK_X:
                            token_x(T + TOK_X[n])
                        if n in TOK_N:
                            token_norm(T + TOK_N[n])
                        if n in TOK_HL:
                            token_low(T + TOK_HL[n])
                    elif n // (NB * HG) < NG - 1:
                        g = n // (NB * HG) + 1
                        for at, f in UV_SLOTS.items():
                            if n % (NB * HG) == at:
                                f(g)

            UV_SLOTS = {
                0: lambda g: uv_make(g, 0), 1: lambda g: uv_make(g, 1),
                3: lambda g: uv_rest(g, 0, False), 4: lambda g: uv_rest(g, 1, False),
                6: lambda g: uv_rest(g, 0, True), 7: lambda g: uv_rest(g, 1, True),
            }
            for at in sorted(UV_SLOTS):
                UV_SLOTS[at](0)
            chunk(0)
            with dve.Fori(1, NC) as c:
                chunk(c)
            for h in (H - 2, H - 1):
                take_sums(NC - 1, h)
            combine(NC - 1, NG - 1)
            def split_lo(u, s, par):
                dve.wait_ge(w_hi_ok, u + 1)
                nc.vector.tensor_tensor(w_lo[par][:, s, :], w_raw[:, s, :], w_hi[par][:, s, :].bitcast(F32),
                                        ALU.subtract).then_inc(w_lo_ok, 1)


            def make_gates():
                G = [0]

                def gstep(ins):
                    ins.then_inc(gate_dve, 1)
                    G[0] += 1
                    dve.wait_ge(gate_dve, G[0])
                b8 = lambda r: top[:, r, :].unsqueeze(2).broadcast_to([P, NT, E])
                dve.wait_ge(const_ok, 1 + E)
                rk = rank[:].unsqueeze(1).broadcast_to([P, NT, E])
                dve.wait_ge(sc_ready, 1)
                gstep(nc.vector.tensor_copy(sc[:], bank[7][:, 0:NT * E].rearrange("p (t e) -> p t e", e=E)))
                gstep(nc.vector.tensor_reduce(top[:, 0, :], sc[:], axis=AX.X, op=ALU.max))
                for r, eq in ((0, eq1), (1, eq2)):
                    gstep(nc.vector.tensor_tensor(eq[:], sc[:], b8(r), ALU.is_equal))
                    gstep(nc.vector.tensor_tensor(eq[:], eq[:], rk, ALU.mult))
                    gstep(nc.vector.tensor_reduce(top[:, 3, :], eq[:], axis=AX.X, op=ALU.max))
                    gstep(nc.vector.tensor_tensor(eq[:], eq[:], b8(3), ALU.is_equal))
                    if r == 0:
                        gstep(nc.vector.scalar_tensor_tensor(sc[:], eq[:], -3.0e38, sc[:], ALU.mult, ALU.add))
                        gstep(nc.vector.tensor_reduce(top[:, 1, :], sc[:], axis=AX.X, op=ALU.max))
                gstep(nc.vector.tensor_tensor(top[:, 2, :], top[:, 1, :], top[:, 0, :], ALU.subtract))
                assert G[0] == GATE_EXP, G[0]
                dve.wait_ge(gate_exp, 1)
                gstep(nc.vector.tensor_scalar(top[:, 4, :], top[:, 2, :], 1.0, None, ALU.add))
                gstep(nc.vector.reciprocal(top[:, 4, :], top[:, 4, :]))
                gstep(nc.vector.tensor_tensor(top[:, 5, :], top[:, 2, :], top[:, 4, :], ALU.mult))
                gstep(nc.vector.tensor_tensor(eq1[:], eq1[:], b8(4), ALU.mult))
                gstep(nc.vector.tensor_tensor(eq2[:], eq2[:], b8(5), ALU.mult))
                gstep(nc.vector.tensor_tensor(gates[:], eq1[:], eq2[:], ALU.add))
                dve.wait_ge(acc_in, 16)

            def last_z_min(k):
                dve.wait_ge(last_proj, k + 1)
                nc.vector.tensor_tensor(z4[:, k, :], bank[4 + k][:], b_row[:], ALU.add).then_inc(last_z, 1)
                dve.wait_ge(last_z, 2 * k + 1)
                nc.vector.tensor_scalar(ez4[:, k, :], z4[:, k, :], 0.0, None, ALU.min).then_inc(last_z, 1)

            def last_x2(k):
                x2 = acc[:, T_LAST + k, :]
                dve.wait_ge(last_exp, k + 1)
                nc.vector.scalar_tensor_tensor(ez4[:, k, :], z4[:, k, :], 0.0, ez4[:, k, :],
                                               ALU.max, ALU.add).then_inc(last_x, 1)
                dve.wait_ge(last_x, 4 * k + 1)
                dve.wait_ge(last_in, 16)
                nc.vector.scalar_tensor_tensor(x2, ez4[:, k, :], -1.0, x2, ALU.add, ALU.add).then_inc(last_x, 1)
                dve.wait_ge(last_x, 4 * k + 2)
                nc.vector.bn_stats(bst4[:, k, :], x2).then_inc(last_x, 1)
                dve.wait_ge(last_x, 4 * k + 3)
                nc.vector.bn_aggr(mv4[:, k, :], bst4[:, k, :]).then_inc(last_x, 1)

            def last_norm():
                dve.wait_ge(last_x, 4 * TPC)
                nc.vector.tensor_scalar(rs4[:, 0, :], mv4[:, :, 1], EPS, None, ALU.add).then_inc(last_x, 1)
                dve.wait_ge(last_rs, 1)
                y, t = rs4[:, 1, :], rs4[:, 2, :]
                nc.vector.tensor_tensor(t, y, y, ALU.mult).then_inc(last_n, 1)
                dve.wait_ge(last_n, 1)
                nc.vector.scalar_tensor_tensor(t, t, -0.5, rs4[:, 0, :], ALU.mult, ALU.mult).then_inc(last_n, 1)
                dve.wait_ge(last_n, 2)
                nc.vector.scalar_tensor_tensor(rs4[:, 3, :], t, 1.5, y, ALU.add, ALU.mult).then_inc(last_n, 1)
                dve.wait_ge(last_n, 3)
                for k in range(TPC):
                    nc.vector.tensor_scalar(xn4[:, k, :], acc[:, T_LAST + k, :], mv4[:, k, 0:1], rs4[:, 3, k:k + 1],
                                            ALU.subtract, ALU.mult).then_inc(last_n, 1)

            def last_lows():
                for k in range(TPC):
                    dve.wait_ge(last_xh, k + 1)
                    o = slice(k * P, (k + 1) * P)
                    nc.vector.tensor_tensor(XL[C_LAST][:, :, o], bank[4 + k][:].rearrange("p (k i) -> p k i", k=KT),
                                            XH[C_LAST][:, :, o].bitcast(F32), ALU.subtract).then_inc(last_low, 1)

            def hidden(S, par):
                for ht in range(GH):
                    n = GH * S + ht
                    dve.wait_ge(silu_ready, n + 1)
                    dve.wait_ge(h2_ready, n + 1)
                    nc.vector.tensor_tensor(act_g[:, ht, :], act_s[:, ht, :], bank[2 * ht + 1][:],
                                            ALU.mult).then_inc(g_ready, 1)
                    dve.wait_ge(g_ready, n + 1 + GH)
                    dve.wait_ge(y_ready, TPC * (S + 1))
                    nc.vector.tensor_copy(h_hi[:, par, ht, :], act_g[:, ht, :]).then_inc(hi_done, 1)
                    dve.wait_ge(hi_done, n + 1)
                    nc.vector.tensor_tensor(h_lo[:, par, ht, :], act_g[:, ht, :], h_hi[:, par, ht, :].bitcast(F32),
                                            ALU.subtract).then_inc(hid_ready, 1)

            def take_y(S, c, e):
                for tt in range(TPC):
                    t = TPC * c + tt
                    dve.wait_ge(y_ready, TPC * S + tt + 1 + 2 * TPC)
                    nc.vector.scalar_tensor_tensor(acc[:, t, :], bank[4 + tt][:], gates[:, t, bass.ds(e, 1)],
                                                   acc[:, t, :], ALU.mult, ALU.add).then_inc(y_used, 1)

            for k in range(TPC):
                if k < GH:
                    split_lo(k, k, 0)
                last_z_min(k)
                if k > 0:
                    last_x2(k - 1)
            last_x2(TPC - 1)
            last_norm()
            hidden(0, 0)
            last_lows()

            def two_groups(i, last):
                for k in range(2 * NC):
                    grp = 2 * i + k // NC
                    S = 2 * NC * i + k
                    if not (last and k == 2 * NC - 1):
                        hidden(S + 1, (k + 1) % 2)
                    if isinstance(i, int) and S == 0:
                        make_gates()
                    take_y(S, k % NC, i // 2 if isinstance(i, int) else i // 2)
                    if k % NC < GH and not (last and k >= NC):
                        split_lo(GH * (grp + 1) + k % NC, k % NC, (k // NC + 1) % 2)

            two_groups(0, False)
            with dve.Fori(1, GROUPS // 2 - 1) as i:
                two_groups(i, False)
            two_groups(GROUPS // 2 - 1, True)

        @block.sync
        def _(sp):
            sp.sem_inc(x2_out, 16)
            sp.sem_inc(xhl_out, 16)
            xv = x.rearrange("(t p) d -> p t d", p=P)
            xtile = x.rearrange("(t p) d -> t p d", p=P)
            for i in range(4):
                sp.dma_start(xall[:, 4 * i:4 * i + 4, :], xv[:, 4 * i:4 * i + 4, :]).then_inc(x_in[i], 16)
                if i == 0:
                    sp.dma_start(a_rows[:, 0, :], a1.partition_broadcast(P)).then_inc(w_in, 16)
                    sp.dma_start(a_rows[:, 1, :], a2.partition_broadcast(P)).then_inc(w_in, 16)
                    sp.dma_start(w_seq[:], W_seq.rearrange("(k p) n -> p k n", p=P)).then_inc(w_in, 16)
                    sp.dma_start(wg[:], WgT.rearrange("(k p) e -> p k e", p=P)).then_inc(w_in, 16)
            sp.wait_ge(su_sTc, NC)
            sp.dma_start(s1_rows.rearrange("(c h) i -> h c i", h=H),
                         s21T[H:2 * H, :].rearrange("h (c i) -> h c i", c=NC)).then_inc(s1_out, 16)
            sp.wait_ge(s1_out, 16)
            sp.wait_ge(su_act, 4)
            sp.wait_ge(su_dve, SU_COLS[0])
            for hh in range(HG):
                sp.dma_start(s1_bc[:, hh, :], s1_rows[hh].partition_broadcast(P)).then_inc(s1_in[hh], 16)

            def load_xt(T):
                sp.wait_ge(x2_out, 16 * T + 16)
                sp.sem_inc(held, 1)
                sp.dma_start(xt[:], xtile[T]).then_inc(xt_in, 16)

            def store_x2(T):
                sp.wait_ge(tok_n, N_ALL * (T + 1))
                sp.sem_inc(held, 1)
                sp.dma_start(x2_dram[T], xt[:]).then_inc(x2_out, 16)

            def store_hl(T, c, k):
                sp.wait_ge(tok_xh, T + 1)
                sp.sem_inc(held, 1)
                sp.wait_ge(tok_low, T + 1)
                sp.sem_inc(held, 1)
                sp.dma_start(xh_dram[c, :, :, k * P:(k + 1) * P], xh[:].bitcast(F32)).then_inc(xhl_out, 16)
                sp.dma_start(xl_dram[c, :, :, k * P:(k + 1) * P], xl[:].bitcast(F32)).then_inc(xhl_out, 16)

            def chunk(c):
                first = isinstance(c, int)
                T = TPC * (c - 1)
                if not first:
                    load_xt(T)
                for h in range(H):
                    sp.wait_ge(mask_ready, SLOTS * c + NB * (h + 1))
                    sp.sem_inc(held, 1)
                    row = (H * c + h + HG) % (NC * H) if h >= H - HG else H * c + h + HG
                    sp.dma_start(s1_bc[:, h % HG, :], s1_rows[row].partition_broadcast(P)).then_inc(s1_in[h % HG], 16)
                    for k in range(TPC):
                        if not first and h == (34 + 8 * k) // NB:
                            store_x2(T + k)
                            if k < TPC - 1:
                                load_xt(T + k + 1)
                        if not first and h == min(41 + 8 * k, SLOTS - 1) // NB:
                            store_hl(T + k, c - 1, k)
                if first:
                    sp.wait_ge(uv_ready, 2 * NG)
                    sp.dma_start(w_out[:], W_out.rearrange("(k p) n -> p k n", p=P)).then_inc(wo_in, 16)
                    sp.dma_start(b_row[:], b_out.partition_broadcast(P)).then_inc(wo_in, 16)

            chunk(0)
            with sp.Fori(1, NC) as c:
                chunk(c)
            sp.wait_ge(x2_out, 16 * T_LAST + 16)
            sp.wait_ge(xhl_out, 32 * T_LAST + 16)
            for u in range(GH):
                sp.dma_start(w_raw[:, u, :], ffn_w[u]).then_inc(raw_in[u], 16)
            sp.wait_ge(comb, HIDDEN_DONE)
            sp.wait_ge(adj_in, 64 * (NC + 1))
            for i in range(HG):
                sp.wait_ge(s1_in[i], 16 * (NC * H // HG + 1))
            sp.dma_start(acc[:, T_LAST:, :], xv[:, T_LAST:, :]).then_inc(last_in, 16)
            for c in range(C_LAST):
                sp.dma_start(XH[c][:].bitcast(F32), xh_dram[c]).then_inc(XT_in[c], 16)
                sp.dma_start(XL[c][:].bitcast(F32), xl_dram[c]).then_inc(XT_in[c], 16)
            sp.dma_start(acc[:, 0:T_LAST, :], x2_dram.rearrange("t p d -> p t d")).then_inc(acc_in, 16)
            with sp.Fori(1, UN // 2) as i:
                for s in range(2):
                    sp.wait_ge(w_hi_ok, 2 * i + s - 1)
                    sp.wait_ge(w_lo_ok, 2 * i + s - 1)
                    sp.sem_inc(held, 1)
                    sp.dma_start(w_raw[:, s, :], ffn_w[2 * i + s]).then_inc(raw_in[s], 16)
            ov = out.rearrange("(t p) d -> p t d", p=P)
            for c in range(NC):
                sp.wait_ge(y_used, TPC * NC * (GROUPS - 1) + TPC * (c + 1) + 4)
                sp.dma_start(ov[:, TPC * c:TPC * (c + 1), :], acc[:, TPC * c:TPC * (c + 1), :]).then_inc(out_done, 16)
            sp.wait_ge(out_done, 16 * NC)

        @block.gpsimd
        def _(pool):
            adj_v = adjT.rearrange("(j p) i -> p j i", p=P)

            def load_adj(c):
                for q in range(4):
                    pool.dma_start(adj_next[:, 4 * q:4 * q + 4, :],
                                   adj_v[:, 4 * q:4 * q + 4, c * CH:(c + 1) * CH]).then_inc(adj_in, 16)

            nc.gpsimd.memset(ident[:], 0.0).then_inc(su_pool, 1)
            nc.gpsimd.memset(ones[:], 1.0).then_inc(su_pool, 1)
            nc.gpsimd.memset(ones_bf[:], 1.0).then_inc(su_pool, 1)
            nc.gpsimd.memset(minus_half[:], -0.5).then_inc(su_pool, 1)
            pool.wait_ge(su_pool, 4)
            nc.gpsimd.affine_select(out=ident[:], in_=ident[:], compare_op=ALU.not_equal, fill=1.0, base=0,
                                    pattern=[[-1, P]], channel_multiplier=1).then_inc(const_ok, 1)
            for q in range(4):
                pool.wait_ge(su_dve, SU_VAR[q])
                nc.gpsimd.tensor_tensor(rs0[:, 1, 4 * q:4 * q + 4], rs0[:, 0, 4 * q:4 * q + 4],
                                        minus_half[:, 0:4], ALU.pow).then_inc(su_pool, 1)
                if q == 0:
                    load_adj(0)

            def rsqrt(T):
                pool.wait_ge(tok_x, X_ALL * (T + 1))
                nc.gpsimd.tensor_tensor(rs[:, 1:2], rs[:, 0:1], minus_half[:, 0:1], ALU.pow).then_inc(tok_rs, 1)

            for c in range(NC):
                pool.wait_ge(adj_ok, 4 * (c + 1))
                load_adj((c + 1) % NC)
                if c > 0:
                    with pool.Fori(TPC * (c - 1), TPC * c) as T:
                        rsqrt(T)
            pool.wait_ge(last_x, LAST_VAR)
            nc.gpsimd.tensor_tensor(rs4[:, 1, :], rs4[:, 0, :], minus_half[:], ALU.pow).then_inc(last_rs, 1)
            for e in range(E):
                nc.gpsimd.memset(rank[:, e:e + 1], float(E - e)).then_inc(const_ok, 1)

        @block.scalar
        def _(act):
            def keep_seq(t):
                act.wait_ge(seq_ready, t + 1)
                nc.scalar.copy(seq[:, t, :], bank[2 + t % 2][:]).then_inc(seq_kept, 1)

            for t in range(NT):
                act.wait_ge(su_tr, t + 1)
                nc.scalar.copy(xT[:, :, t * P:(t + 1) * P],
                               bank[t % 2][:].rearrange("p (k i) -> p k i", k=KT)).then_inc(su_xT, 1)
                if t >= 1:
                    keep_seq(t - 1)
                if t % TPC == TPC - 1:
                    c = t // TPC
                    act.wait_ge(su_sT, c + 1)
                    nc.scalar.copy(s21T[:, c * CH:(c + 1) * CH], bank[4 + c % 2][0:2 * H, :]).then_inc(su_sTc, 1)
            keep_seq(NT - 1)
            act.wait_ge(su_dve, SU_COLS[0])
            nc.scalar.activation(col_B[:], s2c[:], ACT.Exp).then_inc(su_act, 1)
            nc.scalar.activation(col_D[:], s2c[:], ACT.Exp, scale=0.2).then_inc(su_act, 1)
            nc.scalar.activation(row_a[:], ylo[:], ACT.Exp, scale=0.8).then_inc(su_act, 1)
            nc.scalar.activation(row_c[:], y_col[:], ACT.Exp, scale=-0.8).then_inc(su_act, 1)

            TH = NT // 2

            def uv_part(g, half, k):
                n = 2 * g + half
                ts = slice(TH * half, TH * (half + 1))
                act.wait_ge(rest_ready if k else uvf_ready, n + 1)
                nc.scalar.copy(uv[:, ts, HG * g:HG * (g + 1), k * Q2:(k + 1) * Q2],
                               uvf[:, ts]).then_inc(mid_ready if k else hi_ready, 1)

            def relus(c, n):
                h, b = n // NB, n % NB
                if b == 0:
                    act.wait_ge(s1_in[h % HG], 16 * (NG * c + h // HG + 1))
                act.wait_ge(batch_done, SLOTS * c + n + 1)
                act.sem_inc(held, 1)
                for k in range(ON_ACT):
                    last = nc.scalar.activation(mask[:, n % RING, k, :], s1_bc[:, h % HG, :], ACT.Relu, scale=BIG,
                                                bias=s2_big[:, BJ * b + k, h:h + 1], saturate=False)
                last.then_inc(relu_ready, 1)

            def hidT_copy(T, k):
                act.wait_ge(tok_tr1, T + 2)
                nc.scalar.copy(hidT[:, k], (TR, PR)[k % 2][:].rearrange("p (k i) -> p k i", k=KT)).then_inc(tok_hidT, 1)

            def elu_exp(T):
                act.wait_ge(tok_z, Z_ALL * (T + 1))
                nc.scalar.activation(ez[:], ez[:], ACT.Exp).then_inc(tok_exp, 1)

            def xh_copy(T):
                act.wait_ge(tok_tr2, T + 1)
                act.wait_ge(xhl_out, 32 * T + 16)
                nc.scalar.copy(xh[:], TR[:].rearrange("p (k i) -> p k i", k=KT)).then_inc(tok_xh, 1)

            def chunk(c):
                first = isinstance(c, int)
                T = TPC * (c - 1)
                for n in range(SLOTS):
                    relus(c, n)
                    if not first:
                        if n in HIDT:
                            hidT_copy(T + HIDT[n], HIDT[n])
                        if n in TOK_EXP:
                            elu_exp(T + TOK_EXP[n])
                        if n in TOK_HL:
                            xh_copy(T + TOK_HL[n])
                    elif n // (NB * HG) < NG - 1:
                        g = n // (NB * HG) + 1
                        for at, half, k in ((1, 0, 0), (2, 1, 0), (4, 0, 1), (5, 1, 1)):
                            if n % (NB * HG) == at:
                                uv_part(g, half, k)

            for k in range(2):
                for half in range(2):
                    uv_part(0, half, k)
            chunk(0)
            with act.Fori(1, NC) as c:
                chunk(c)
            def split_hi(grp, s, par):
                act.wait_ge(raw_in[s], 16 * (grp + 1))
                if not isinstance(grp, int) or grp > 0:
                    act.wait_ge(y_ready, TPC * NC * (grp - 1) + 2 * TPC)
                nc.scalar.copy(w_hi[par][:, s, :], w_raw[:, s, :]).then_inc(w_hi_ok, 1)

            def silu(S):
                for ht in range(GH):
                    n = GH * S + ht
                    act.wait_ge(h1_ready, n + 1)
                    act.wait_ge(g_ready, n + 1)
                    nc.scalar.activation(act_s[:, ht, :], bank[2 * ht][:], ACT.Silu).then_inc(silu_ready, 1)

            for k in range(TPC):
                act.wait_ge(last_tr1, k + 1)
                nc.scalar.copy(hidT[:, k], bank[4 + k][:].rearrange("p (k i) -> p k i", k=KT)).then_inc(last_hidT, 1)
            for i in range(HG):
                act.wait_ge(s1_in[i], 16 * (NC * H // HG + 1))
            for u in range(GH):
                split_hi(0, u, 0)
            for k in range(TPC):
                act.wait_ge(last_z, 2 * (k + 1))
                nc.scalar.activation(ez4[:, k, :], ez4[:, k, :], ACT.Exp).then_inc(last_exp, 1)

            def keep_scores(c):
                act.wait_ge(row_ready, c + 1)
                nc.scalar.copy(scT[:, c * CH:(c + 1) * CH], bank[4 + c % 2][0:E, :]).then_inc(row_kept, 1)

            silu(0)
            for c in range(2):
                keep_scores(c)
            for k in range(TPC):
                act.wait_ge(last_tr2, k + 1)
                nc.scalar.copy(XH[C_LAST][:, :, k * P:(k + 1) * P],
                               bank[4 + k][:].rearrange("p (k i) -> p k i", k=KT)).then_inc(last_xh, 1)

            def two_groups(i, last):
                for k in range(2 * NC):
                    grp = 2 * i + k // NC
                    S = 2 * NC * i + k
                    if not (last and k == 2 * NC - 1):
                        silu(S + 1)
                    if isinstance(i, int) and S == 0:
                        for c in range(2, NC):
                            keep_scores(c)
                        act.wait_ge(gate_dve, GATE_EXP)
                        nc.scalar.activation(top[:, 2, :], top[:, 2, :], ACT.Exp).then_inc(gate_exp, 1)
                    if k % NC < GH and not (last and k >= NC):
                        split_hi(grp + 1, k % NC, (k // NC + 1) % 2)

            two_groups(0, False)
            with act.Fori(1, GROUPS // 2 - 1) as i:
                two_groups(i, False)
            two_groups(GROUPS // 2 - 1, True)

        @block.tensor
        def _(pe):
            mm = nc.tensor.matmul
            pe.sem_inc(batch_done, RING)
            pe.sem_inc(sums_free, 2)
            pe.sem_inc(av_free, 2)
            pe.sem_inc(tok_tr1, 1)
            pe.sem_inc(g_ready, GH)
            pe.sem_inc(y_ready, 2 * TPC)
            pe.sem_inc(y_used, TPC)

            pe.wait_ge(const_ok, 1)

            def project_seq(t):
                pe.wait_ge(su_xT, t + 1)
                if t >= 2:
                    pe.wait_ge(seq_kept, t - 1)
                for k in range(KT):
                    last = mm(bank[2 + t % 2][:], xT[:, k, t * P:(t + 1) * P], w_seq[:, k, :],
                              start=(k == 0), stop=(k == KT - 1))
                last.then_inc(seq_ready, 1)

            def score_rows(c):
                pe.wait_ge(su_dve, SU_W12[0])
                if c >= 2:
                    pe.wait_ge(su_sTc, c - 1)
                for k in range(KT):
                    last = mm(bank[4 + c % 2][0:2 * H, :], w12[:, k, :], xT[:, k, c * CH:(c + 1) * CH],
                              start=(k == 0), stop=(k == KT - 1))
                last.then_inc(su_sT, 1)

            pe.wait_ge(w_in, 64)
            for t in range(NT):
                pe.wait_ge(su_dve, SU_XN[t])
                if t >= 2:
                    pe.wait_ge(su_xT, t - 1)
                for k in range(KT):
                    last = nc.tensor.transpose(bank[t % 2][:, k * P:(k + 1) * P], xall[:, t, k * P:(k + 1) * P], ident[:])
                last.then_inc(su_tr, 1)
                if t >= 1:
                    project_seq(t - 1)
                if t % TPC == TPC - 1:
                    pe.wait_ge(su_xT, t + 1)
                    score_rows(t // TPC)
            project_seq(NT - 1)
            pe.wait_ge(su_sTc, NC)
            for t in range(NT):
                last = nc.tensor.transpose(bank[0][:, t * 2 * H:(t + 1) * 2 * H], s21T[:, t * P:(t + 1) * P],
                                           ident[0:2 * H, 0:2 * H])
            last.then_inc(su_cols, 1)
            pe.wait_ge(su_dve, SU_DIAG[0])
            mm(bank[1][:, 0:H], ones[0:H, :], gdiag[:], start=True, stop=True).then_inc(su_g, 1)

            def degrees(c):
                pe.wait_ge(adj_in, 64 * (c + 1))
                pe.sem_inc(held, 1)
                for j in range(NT):
                    last = mm(PR[:], ones_bf[:], adj_next[:, j, :], start=(j == 0), stop=(j == NT - 1))
                last.then_inc(deg_ready, 1)

            def head_batch(c, n):
                h, b = n // NB, n % NB
                if b == 0:
                    pe.wait_ge(sums_free, H * c + h + 1)
                pe.wait_ge(mask_ready, SLOTS * c + n + 1)
                pe.sem_inc(held, 1)
                for k in range(BJ):
                    j = BJ * b + k
                    for t in range(TPC):
                        o = (t % 2) * PARTS * Q2
                        last = mm(bank[2 * (h % 2) + t // 2][:, o:o + PARTS * Q2],
                                  mask[:, n % RING, k, t * P:(t + 1) * P], uv[:, j, h, :],
                                  start=(j == 0 and t % 2 == 0), stop=(j == NT - 1), skip_group_check=True)
                last.then_inc(batch_done, 1)

            def adj_v(c, n):
                for m in range(AVS * n, min(AVS * (n + 1), NT * NT)):
                    p, j = m // NT, m % NT
                    g, t = p // TPC, p % TPC
                    if j == 0:
                        pe.wait_ge(av_free, NT * c + p + 1)
                        pe.sem_inc(held, 1)
                        if t == 0 and isinstance(c, int):
                            pe.wait_ge(uv_ready, 2 * (g + 1))
                    rhs = uv[:, j, HG * g:HG * (g + 1), :].rearrange("p h (r q) -> p h r q", r=PARTS)[:, :, :, Q:Q2]
                    mm_ = mm(bank[4 + p % 2][:, 0:HG * PARTS * Q], adj[:, j, t * P:(t + 1) * P], rhs,
                             start=(j == 0), stop=(j == NT - 1))
                    if j == NT - 1:
                        mm_.then_inc(av_ready, 1)

            def tok_transpose(T, k):
                if k >= 2:
                    pe.wait_ge(tok_hidT, T - 1)
                for q in range(KT):
                    last = nc.tensor.transpose((TR, PR)[k % 2][:, q * P:(q + 1) * P], hid[:, k, q * P:(q + 1) * P], ident[:])
                last.then_inc(tok_tr1, 1)

            def tok_project(T, k):
                for q in range(KT):
                    last = mm(PR[:], hidT[:, k, q, :], w_out[:, q, :], start=(q == 0), stop=(q == KT - 1))
                last.then_inc(tok_proj, 1)

            def tok_transpose2(T):
                pe.wait_ge(tok_n, N_ALL * (T + 1))
                for k in range(KT):
                    last = nc.tensor.transpose(TR[:, k * P:(k + 1) * P], xn[:, k * P:(k + 1) * P], ident[:])
                last.then_inc(tok_tr2, 1)

            def chunk(c):
                first = isinstance(c, int)
                T = TPC * (c - 1)
                pe.wait_ge(adj_ok, 4 * (c + 1))
                for n in range(SLOTS):
                    if first and n % (NB * HG) == 0:
                        pe.wait_ge(uv_ready, 2 * (n // (NB * HG) + 1))
                    head_batch(c, n)
                    adj_v(c, n)
                    if not first:
                        if n in TR1:
                            if TR1[n] == 0:
                                pe.wait_ge(comb, C_ALL * NG * c)
                            tok_transpose(T + TR1[n], TR1[n])
                        if n in PROJ:
                            if PROJ[n] == 0:
                                pe.wait_ge(tok_hidT, T + TPC)
                            else:
                                pe.wait_ge(tok_z, Z_ALL * (T + PROJ[n]))
                            tok_project(T, PROJ[n])
                        if n in TR2:
                            if TR2[n] > 0:
                                pe.wait_ge(tok_low, T + TR2[n])
                            tok_transpose2(T + TR2[n])
                    if n == DEGREES:
                        if not first:
                            pe.wait_ge(tok_z, Z_ALL * (T + TPC))
                        degrees(c + 1)
                if first:
                    pe.wait_ge(wo_in, 32)

            degrees(0)
            chunk(0)
            with pe.Fori(1, NC) as c:
                chunk(c)
            def three(out_, hi, lo, rhi, rlo, start, stop):
                mm(out_, hi, rhi, start=start, stop=False)
                mm(out_, hi, rlo, start=False, stop=False)
                return mm(out_, lo, rhi, start=False, stop=stop)

            def up(S, grp, par, c):
                if c == 0:
                    pe.wait_ge(w_hi_ok, GH * (grp + 1))
                    pe.wait_ge(w_lo_ok, GH * (grp + 1))
                if c < C_LAST:
                    pe.wait_ge(XT_in[c], 32)
                for ht in range(GH):
                    pe.wait_ge(g_ready, GH * S + ht + 1)
                    for s, done in ((0, h1_ready), (1, h2_ready)):
                        for k in range(KT):
                            o = s * D + k * P
                            last = three(bank[2 * ht + s][:], w_hi[par][:, ht, o:o + P], w_lo[par][:, ht, o:o + P],
                                         XH[c][:, k, :], XL[c][:, k, :], k == 0, k == KT - 1)
                        last.then_inc(done, 1)

            def down(S, grp, par, hpar, c):
                pe.wait_ge(hid_ready, GH * (S + 1))
                for tt in range(TPC):
                    pe.wait_ge(y_used, TPC * S + tt + 1)
                    if isinstance(S, int) and S == 0 and tt == TPC - 1:
                        pe.wait_ge(gate_dve, 1)
                    for ht in range(GH):
                        last = three(bank[4 + tt][:], h_hi[:, hpar, ht, tt * P:(tt + 1) * P],
                                     h_lo[:, hpar, ht, tt * P:(tt + 1) * P],
                                     w_hi[par][:, ht, 2 * D:], w_lo[par][:, ht, 2 * D:], ht == 0, ht == GH - 1)
                    last.then_inc(y_ready, 1)

            def score_rows_of(c):
                if c < C_LAST:
                    pe.wait_ge(XT_in[c], 32)
                    pe.wait_ge(last_z, 2 * (c % 2 + 1))
                else:
                    pe.wait_ge(last_low, TPC)
                if c >= 2:
                    pe.wait_ge(last_low, c % 2 + 1)
                for k in range(KT):
                    last = three(bank[4 + c % 2][0:E, :], wg_hi[:, k, :], wg_lo[:, k, :],
                                 XH[c][:, k, :], XL[c][:, k, :], k == 0, k == KT - 1)
                last.then_inc(row_ready, 1)

            def score_columns():
                pe.wait_ge(last_low, TPC)
                pe.wait_ge(row_kept, NC)
                for t in range(NT):
                    last = nc.tensor.transpose(bank[7][:, t * E:(t + 1) * E], scT[:, t * P:(t + 1) * P], ident[0:E, 0:E])
                last.then_inc(sc_ready, 1)

            pe.wait_ge(comb, HIDDEN_DONE)
            for k in range(TPC):
                for q in range(KT):
                    last = nc.tensor.transpose(bank[4 + k][:, q * P:(q + 1) * P], hid[:, k, q * P:(q + 1) * P], ident[:])
                last.then_inc(last_tr1, 1)
            for k in range(TPC):
                pe.wait_ge(last_hidT, k + 1)
                for q in range(KT):
                    last = mm(bank[4 + k][:], hidT[:, k, q, :], w_out[:, q, :], start=(q == 0), stop=(q == KT - 1))
                last.then_inc(last_proj, 1)
            up(0, 0, 0, 0)
            score_rows_of(0)
            score_rows_of(1)
            for k in range(TPC):
                pe.wait_ge(last_n, 3 + k + 1)
                if k < 2:
                    pe.wait_ge(row_kept, k + 1)
                for q in range(KT):
                    last = nc.tensor.transpose(bank[4 + k][:, q * P:(q + 1) * P], xn4[:, k, q * P:(q + 1) * P], ident[:])
                last.then_inc(last_tr2, 1)

            def two_groups(i, last):
                for k in range(2 * NC):
                    grp = 2 * i + k // NC
                    S = 2 * NC * i + k
                    if not (last and k == 2 * NC - 1):
                        k1 = k + 1
                        up(S + 1, 2 * i + k1 // NC, (k1 // NC) % 2, k1 % NC)
                    if isinstance(i, int) and S == 0:
                        score_rows_of(2)
                        score_rows_of(3)
                        score_columns()
                    down(S, grp, (k // NC) % 2, k % 2, k % NC)

            two_groups(0, False)
            with pe.Fori(1, GROUPS // 2 - 1) as i:
                two_groups(i, False)
            two_groups(GROUPS // 2 - 1, True)


def kernel(**inputs):
    import numpy as np
    import concourse.bacc as bacc
    from concourse.bass_utils import run_bass_kernel_spmd

    a = {k: np.asarray(v) for k, v in inputs.items()}

    def up_layout(w):
        return w.reshape(E, HID // P, P, KT, P).transpose(0, 1, 4, 3, 2).reshape(UN, P, D)

    w3 = a["L0_ffn_W3"].reshape(E, D, HID // P, P).transpose(0, 2, 3, 1).reshape(UN, P, D)
    arrays = {
        "x": a["x"], "adjT": a["adj"].T, "W_seq": a["L0_gnn_W_seq"], "a1": a["L0_gnn_a1"], "a2": a["L0_gnn_a2"],
        "W_out": a["L0_gnn_W_out"], "b_out": a["L0_gnn_b_out"], "WgT": a["L0_ffn_Wg"].T,
        "ffn_w": np.concatenate([up_layout(a["L0_ffn_W1"]), up_layout(a["L0_ffn_W2"]), w3], axis=2),
    }
    arrays = {k: np.ascontiguousarray(v) for k, v in arrays.items()}
    nc = bacc.Bacc("TRN2", target_bir_lowering=False, num_devices=1, dynamic_dma_scratch_size=4096)
    args = [nc.dram_tensor(k, v.shape, mybir.dt.from_np(v.dtype), kind="ExternalInput").ap() for k, v in arrays.items()]
    args.append(nc.dram_tensor("out", (N, D), F32, kind="ExternalOutput").ap())
    build(nc, *args)
    r = run_bass_kernel_spmd(nc, [arrays], core_ids=[0])
    return r.results[0]["out"]
```

```python
import concourse.bass as bass
from concourse import mybir
from contextlib import ExitStack

F32 = mybir.dt.float32
F32R = mybir.dt.float32r
F8 = mybir.dt.float8e5
U8 = mybir.dt.uint8
BF16 = mybir.dt.bfloat16
I32 = mybir.dt.int32
ALU = mybir.AluOpType
ACT = mybir.ActivationFunctionType
AX = mybir.AxisListType

P = 128
N, D = 2048, 512
H, DH = 16, 32
E, HID = 8, 1024
KT = D // P
NT = N // P
CH = 512
NC = N // CH
TPC = CH // P
Q = DH + 1
Q2 = 2 * Q
PARTS = 3
EPS = 1e-5
BIG = float(2 ** 60)

HG = 4
NG = H // HG
UT = 4
UPG = NT // UT
BJ = 4
NB = NT // BJ
SLOTS = NB * H
RING = 8
ON_ACT = 3
ONE8 = 0x3C
ODD = BJ - 1
AVJ = NT - NB
AV_SLOTS = 57

TILE_BYTES = 6 * D * 4
XT_REST = (KT * N + KT * D - TPC * D - KT * D - D) * 4 - TILE_BYTES
SETUP_AT = (TILE_BYTES + XT_REST + 2 * UT * HG * Q2 * 4 + 2 * NT * H * 4 + 2 * NT * CH
            + NT * H * PARTS * Q2 * 2 + 4 * NT * H * 4)
UN = E * HID // P
GH = 2
GROUPS = UN // GH
WU = 2 * KT * P + D


def build(nc, x, adjT, W_seq, a1, a2, W_out, b_out, WgT, ffn_w, out):
    ctx = ExitStack()
    with ctx:
        def keep(name, shape, dt, where=None):
            return (where or ctx).enter_context(nc.sbuf_tensor(name, shape, dt))

        def sem(name):
            return ctx.enter_context(nc.semaphore(name))

        s1_rows = nc.dram_tensor("s1_rows", [NC * H, CH], F32, kind="Internal").ap()
        x2_dram = nc.dram_tensor("x2_dram", [NT - TPC, P, D], F32, kind="Internal").ap()
        xh_dram = nc.dram_tensor("xh_dram", [NC - 1, P, KT, CH], F32, kind="Internal").ap()
        xl_dram = nc.dram_tensor("xl_dram", [NC - 1, P, KT, CH], F32, kind="Internal").ap()

        ident = keep("ident", [P, P], F32)
        ones = keep("ones", [P, P], F32)
        ones_bf = keep("ones_bf", [P, P], BF16)
        wg = keep("wg", [P, KT, E], F32)
        wg_hi = keep("wg_hi", [P, KT, E], F32R)
        wg_lo = keep("wg_lo", [P, KT, E], F32R)
        gates = keep("gates", [P, NT, E], F32)
        minus_half = keep("minus_half", [P, TPC], F32)

        bank = [ctx.enter_context(nc.psum_tensor(f"bank{i}", [P, 512], F32)) for i in range(8)]

        bst = keep("bst", [P, 6], F32)
        mv = keep("mv", [P, 2], F32)
        rs = keep("rs", [P, 4], F32)
        bst4 = keep("bst4", [P, TPC, 6], F32)
        mv4 = keep("mv4", [P, TPC, 2], F32)
        rs4 = keep("rs4", [P, 4, TPC], F32)
        hid = keep("hid", [P, TPC, D], F32)
        X1 = ExitStack()
        xT = keep("xT", [P, KT, N], F32, X1)
        w_seq = keep("w_seq", [P, KT, D], F32, X1)
        X1.close()
        hidT = keep("hidT", [P, TPC, KT, P], F32)
        w_out = keep("w_out", [P, KT, D], F32)
        b_row = keep("b_row", [P, D], F32)
        A = ExitStack()
        z = keep("z", [P, D], F32, A)
        ez = keep("ez", [P, D], F32, A)
        xt = keep("xt", [P, D], F32, A)
        xn = keep("xn", [P, D], F32, A)
        xh = keep("xh", [P, KT, P], F32R, A)
        xl = keep("xl", [P, KT, P], F32R, A)
        keep("rest_of_xT", [P, XT_REST], U8, A)
        uvf = keep("uvf", [P, 2, UT, HG, Q2], F32, A)
        col_B = keep("col_B", [P, NT, H], F32, A)
        col_D = keep("col_D", [P, NT, H], F32, A)
        adj = keep("adj", [P, NT, CH], F8, A)
        adj_next = keep("adj_next", [P, NT, CH], F8, A)
        X0 = ExitStack()
        xall = keep("xall", [P, NT, D], F32, X0)
        wtmp = keep("wtmp", [P, KT * H, DH], F32, X0)
        a_rows = keep("a_rows", [P, 2, DH], F32, X0)
        X0.close()
        uv = keep("uv", [P, NT, H, PARTS * Q2], BF16, A)
        s2_big = keep("s2_big", [P, NT, H], F32, A)
        s2_neg = keep("s2_neg", [P, NT, H], F32, A)
        row_a = keep("row_a", [P, NT, H], F32, A)
        row_c = keep("row_c", [P, NT, H], F32, A)
        s1_bc = keep("s1_bc", [P, HG, CH], F32, A)
        mask = keep("mask", [P, RING, BJ + 1, CH], F8, A)
        sums = keep("sums", [P, TPC, HG, Q2], F32, A)
        av = keep("av", [P, 2, TPC, HG, Q], F32, A)
        rden = keep("rden", [P, TPC, HG], F32, A)
        empty = keep("empty", [P, CH], U8, A)
        A.close()
        X2 = ExitStack()
        keep("below", [P, SETUP_AT], U8, X2)
        w12 = keep("w12", [P, KT, 2 * H], F32, X2)
        s21T = keep("s21T", [2 * H, N], F32, X2)
        gmax4 = keep("gmax4", [H, NC], F32, X2)
        gmax = keep("gmax", [H, 1], F32, X2)
        gdiag = keep("gdiag", [H, H], F32, X2)
        gcol = keep("gcol", [P, H], F32, X2)
        y_col = keep("y_col", [P, NT, H], F32, X2)
        ylo = keep("ylo", [P, NT, H], F32, X2)
        s2c = keep("s2c", [P, NT, H], F32, X2)
        bst0 = keep("bst0", [P, NT, 6], F32, X2)
        mv0 = keep("mv0", [P, NT, 2], F32, X2)
        rs0 = keep("rs0", [P, 4, NT], F32, X2)
        X2.close()

        B = ctx
        w_raw = keep("w_raw", [P, 2, WU], F32, B)
        w_hi, w_lo = [keep("w_hi0", [P, GH, WU], F32R, B)], [keep("w_lo0", [P, GH, WU], F32R, B)]
        X3 = ExitStack()
        z4 = keep("z4", [P, TPC, D], F32, X3)
        ez4 = keep("ez4", [P, TPC, D], F32, X3)
        xn4 = keep("xn4", [P, TPC, D], F32, X3)
        X3.close()
        w_hi.append(keep("w_hi1", [P, GH, WU], F32R, B))
        w_lo.append(keep("w_lo1", [P, GH, WU], F32R, B))
        h_hi = keep("h_hi", [P, 2, GH, CH], F32R, B)
        h_lo = keep("h_lo", [P, 2, GH, CH], F32R, B)
        act_s = keep("act_s", [P, GH, CH], F32, B)
        act_g = keep("act_g", [P, GH, CH], F32, B)
        XH = [keep(f"XH{c}", [P, KT, CH], F32R, B) for c in range(NC)]
        XL = [keep(f"XL{c}", [P, KT, CH], F32R, B) for c in range(NC)]
        acc = keep("acc", [P, NT, D], F32, B)
        scT = keep("scT", [E, N], F32, B)
        sc = keep("sc", [P, NT, E], F32, B)
        eq1 = keep("eq1", [P, NT, E], F32, B)
        eq2 = keep("eq2", [P, NT, E], F32, B)
        rank = keep("rank", [P, E], F32, B)
        top = keep("top", [P, 6, NT], F32, B)

        x_in = [sem(f"x_in{i}") for i in range(4)]
        w_in = sem("w_in")
        wo_in = sem("wo_in")
        s1_out = sem("s1_out")
        adj_in = sem("adj_in")
        s1_in = [sem(f"s1_in{i}") for i in range(HG)]
        xt_in = sem("xt_in")
        x2_out = sem("x2_out")
        xhl_out = sem("xhl_out")
        raw_in = [sem(f"raw_in{i}") for i in range(2)]
        XT_in = [sem(f"XT_in{c}") for c in range(NC - 1)]
        acc_in = sem("acc_in")
        last_in = sem("last_in")
        out_done = sem("out_done")
        const_ok = sem("const_ok")
        su_dve = sem("su_dve")
        su_act = sem("su_act")
        su_pool = sem("su_pool")
        su_tr = sem("su_tr")
        su_xT = sem("su_xT")
        su_sT = sem("su_sT")
        su_sTc = sem("su_sTc")
        su_cols = sem("su_cols")
        su_g = sem("su_g")
        odd_ready = sem("odd_ready")
        seq_ready = sem("seq_ready")
        seq_used = sem("seq_used")
        hi_ready = sem("hi_ready")
        rest_ready = sem("rest_ready")
        mid_ready = sem("mid_ready")
        uv_ready = sem("uv_ready")
        held = sem("held")
        relu_ready = sem("relu_ready")
        cmp_ready = sem("cmp_ready")
        and_ready = sem("and_ready")
        mask_ready = sem("mask_ready")
        batch_done = sem("batch_done")
        sums_free = sem("sums_free")
        av_ready = sem("av_ready")
        av_free = sem("av_free")
        deg_ready = sem("deg_ready")
        empty_ready = sem("empty_ready")
        adj_ok = sem("adj_ok")
        comb = sem("comb")
        tok_tr1 = sem("tok_tr1")
        tok_hidT = sem("tok_hidT")
        tok_proj = sem("tok_proj")
        tok_z = sem("tok_z")
        tok_exp = sem("tok_exp")
        tok_x = sem("tok_x")
        tok_rs = sem("tok_rs")
        tok_n = sem("tok_n")
        tok_tr2 = sem("tok_tr2")
        tok_xh = sem("tok_xh")
        tok_low = sem("tok_low")
        last_tr1 = sem("last_tr1")
        last_hidT = sem("last_hidT")
        last_proj = sem("last_proj")
        last_z = sem("last_z")
        last_exp = sem("last_exp")
        last_x = sem("last_x")
        last_rs = sem("last_rs")
        last_n = sem("last_n")
        last_tr2 = sem("last_tr2")
        last_xh = sem("last_xh")
        last_low = sem("last_low")
        w_hi_ok = sem("w_hi_ok")
        w_lo_ok = sem("w_lo_ok")
        h1_ready = sem("h1_ready")
        h2_ready = sem("h2_ready")
        silu_ready = sem("silu_ready")
        g_ready = sem("g_ready")
        hi_done = sem("hi_done")
        hid_ready = sem("hid_ready")
        y_ready = sem("y_ready")
        y_used = sem("y_used")
        row_ready = sem("row_ready")
        row_kept = sem("row_kept")
        sc_ready = sem("sc_ready")
        gate_dve = sem("gate_dve")
        gate_exp = sem("gate_exp")

        Z_ALL, X_ALL, N_ALL, C_ALL = 2, 5, 4, 6
        TR, PR = bank[6], bank[7]
        C_LAST, T_LAST = NC - 1, NT - TPC
        HIDDEN_DONE = C_ALL * NG * NC
        LAST_VAR = 4 * TPC + 1
        V32 = lambda ap: ap.bitcast(I32)

        TAKE = {NB * h + NB - 1 + 6: h for h in range(H)}
        AV_FROM = [AVJ * NT * min(n, AV_SLOTS) // AV_SLOTS for n in range(SLOTS + 1)]
        AV_DONE = [min(n for n in range(SLOTS) if AV_FROM[n + 1] >= AVJ * (p + 1)) for p in range(NT)]
        TAKE_AV = {t + 6: p for p, t in enumerate(AV_DONE)}
        COMBINE = {NB * HG * (g + 1) - 1 + 7: g for g in range(NG)}
        TR1 = {8: 0, 9: 1, 15: 2, 16: 3}
        HIDT = {14: 0, 15: 1, 21: 2, 22: 3}
        PROJ = {19 + 8 * k: k for k in range(TPC)}
        TOK_Z = {at + 9: k for at, k in PROJ.items()}
        TOK_EXP = {at + 1: k for at, k in TOK_Z.items()}
        TOK_X = {at + 2: k for at, k in TOK_Z.items()}
        TOK_N = {at + 4: k for at, k in TOK_Z.items()}
        TR2 = {at + 4: k for at, k in TOK_Z.items()}
        TOK_HL = {at + 20: k for at, k in PROJ.items()}
        DEGREES = 57
        MAKE_AT = {n: AV_SLOTS * (n - UPG) // NT + 2 for n in range(UPG, UPG * NG)}
        SEQ = {at - 6: n for n, at in MAKE_AT.items()}
        MAKE_AT.update({UPG - 2: 0, UPG - 1: 1})
        MAKE = {at: n for n, at in MAKE_AT.items()}
        HI = REST = {at + 1: n for n, at in MAKE_AT.items()}
        MID = LOW = {at + 2: n for n, at in MAKE_AT.items()}

        def seq_bank(n):
            return bank[(2, 6, 3, 5)[n]] if n < UPG else bank[6 + n % 2]

        def unit(n):
            g, q = n // UPG, n % UPG
            return slice(UT * q, UT * (q + 1)), slice(HG * g, HG * (g + 1))

        block = ctx.enter_context(nc.Block())

        SU_VAR, SU_XN, SU_DIAG, SU_COLS, SU_W12 = [0] * 4, [0] * NT, [0], [0], [0]
        GATE_EXP = 13

        SU = [0]

        def setup_vector(dve):
            def step(ins, wait=None):
                ins.then_inc(su_dve, 1)
                SU[0] += 1
                return SU[0]

            def settle():
                dve.wait_ge(su_dve, SU[0])

            for q in range(4):
                dve.wait_ge(x_in[q], 16)
                ts = range(4 * q, 4 * q + 4)
                for t in ts:
                    step(nc.vector.bn_stats(bst0[:, t, :], xall[:, t, :]))
                settle()
                for t in ts:
                    step(nc.vector.bn_aggr(mv0[:, t, :], bst0[:, t, :]))
                settle()
                qs = slice(4 * q, 4 * q + 4)
                SU_VAR[q] = step(nc.vector.tensor_scalar(rs0[:, 0, qs], mv0[:, qs, 1], EPS, None, ALU.add))
                dve.wait_ge(su_pool, 5 + q)
                newton(dve, rs0[:, 0, qs], rs0[:, 1, qs], rs0[:, 2, qs], step, settle)
                settle()
                for t in ts:
                    SU_XN[t] = step(nc.vector.tensor_scalar(xall[:, t, :], xall[:, t, :], mv0[:, t, 0:1],
                                                            rs0[:, 1, t:t + 1], ALU.subtract, ALU.mult))
                if q == 0:
                    score_weights(dve, step, settle)
            for c in range(NC):
                dve.wait_ge(su_sTc, c + 1)
                step(nc.vector.reduce_max(gmax4[:, c:c + 1], s21T[0:H, c * CH:(c + 1) * CH], axis=AX.X))
            settle()
            step(nc.vector.reduce_max(gmax[:], gmax4[:], axis=AX.X))
            settle()
            SU_DIAG[0] = step(nc.vector.tensor_scalar(gdiag[:], ident[0:H, 0:H], gmax[:, 0:1], None, ALU.mult))
            dve.wait_ge(su_g, 1)
            step(nc.vector.tensor_copy(gcol[:], bank[1][:, 0:H]))
            settle()
            gb = gcol[:].unsqueeze(1).broadcast_to([P, NT, H])
            cols = bank[0][:].rearrange("p (t s) -> p t s", t=NT)
            dve.wait_ge(su_cols, 1)
            step(nc.vector.tensor_tensor(s2c[:], cols[:, :, 0:H], gb, ALU.subtract))
            step(nc.vector.tensor_tensor(y_col[:], cols[:, :, H:2 * H], gb, ALU.add))
            step(nc.vector.tensor_scalar(s2_big[:], cols[:, :, 0:H], BIG, None, ALU.mult))
            step(nc.vector.tensor_scalar(s2_neg[:], cols[:, :, 0:H], -1.0, None, ALU.mult))
            settle()
            step(nc.vector.tensor_scalar(ylo[:], y_col[:], 0.0, None, ALU.min))
            settle()
            SU_COLS[0] = step(nc.vector.tensor_scalar(y_col[:], y_col[:], 0.0, None, ALU.max))

        def score_weights(dve, step, settle):
            dve.wait_ge(w_in, 64)
            wv = w_seq[:].rearrange("p k (h d) -> p (k h) d", d=DH)
            for s in range(2):
                settle()
                step(nc.vector.tensor_tensor(wtmp[:], wv, a_rows[:, 1 - s, :].unsqueeze(1).broadcast_to([P, KT * H, DH]),
                                             ALU.mult))
                settle()
                step(nc.vector.tensor_reduce(w12[:, :, s * H:(s + 1) * H],
                                             wtmp[:].rearrange("p (k h) d -> p k h d", k=KT),
                                             axis=AX.X, op=ALU.add))
            step(nc.vector.tensor_copy(wg_hi[:], wg[:]))
            settle()
            step(nc.vector.tensor_tensor(wg_lo[:], wg[:], wg_hi[:].bitcast(F32), ALU.subtract))
            SU_W12[0] = SU[0]

        def newton(dve, v, y, t, step, settle):
            step(nc.vector.tensor_tensor(t, y, y, ALU.mult))
            settle()
            step(nc.vector.tensor_tensor(t, t, v, ALU.mult))
            settle()
            step(nc.vector.tensor_scalar(t, t, -0.5, 1.5, ALU.mult, ALU.add))
            settle()
            step(nc.vector.tensor_tensor(y, y, t, ALU.mult))

        @block.vector
        def _(dve):
            dve.wait_ge(const_ok, 1)
            setup_vector(dve)
            def uv_make(n):
                ts, hs = unit(n)
                if n == 0:
                    dve.wait_ge(su_act, 4)
                    odd = col_D[:].rearrange("p (b k) h -> p b k h", k=BJ)[:, :, ODD, :]
                    nc.vector.tensor_scalar(odd, odd, -1.0, None, ALU.mult).then_inc(odd_ready, 1)
                    dve.wait_ge(odd_ready, 1)
                if n >= 2:
                    dve.wait_ge(uv_ready, n - 1)
                dve.wait_ge(seq_ready, n + 1)
                u = uvf[:, n % 2]
                sv = seq_bank(n)[:].rearrange("p (t h d) -> p t h d", t=UT, h=HG)
                for s, f in ((0, col_B), (1, col_D)):
                    nc.vector.tensor_copy(u[:, :, :, s * Q + DH], f[:, ts, hs])
                    last = nc.vector.tensor_tensor(u[:, :, :, s * Q:s * Q + DH], sv,
                                                   f[:, ts, hs].unsqueeze(3).broadcast_to([P, UT, HG, DH]), ALU.mult)
                last.then_inc(seq_used, 1)

            def uv_rest(n, low):
                part = uv[:, unit(n)[0], unit(n)[1], :]
                k = 1 if low else 0
                dve.wait_ge(mid_ready if low else hi_ready, n + 1)
                out_ = part[:, :, :, 2 * Q2:] if low else uvf[:, n % 2]
                nc.vector.tensor_tensor(out_, uvf[:, n % 2], part[:, :, :, k * Q2:(k + 1) * Q2],
                                        ALU.subtract).then_inc(uv_ready if low else rest_ready, 1)

            def fix_adj(c):
                dve.wait_ge(deg_ready, c + 1)
                nc.vector.tensor_scalar(empty[:], PR[:], 0.0, float(ONE8), ALU.is_equal, ALU.mult).then_inc(empty_ready, 1)
                if not isinstance(c, int):
                    dve.wait_ge(av_ready, NT * c)
                dve.wait_ge(empty_ready, c + 1)
                for q in range(4):
                    js = slice(4 * q, 4 * q + 4)
                    nc.vector.tensor_tensor(V32(adj[:, js, :]), V32(adj_next[:, js, :]),
                                            V32(empty[:]).unsqueeze(1).broadcast_to([P, 4, CH // 4]),
                                            ALU.bitwise_or).then_inc(adj_ok, 1)

            def masks(c, n):
                h, b = n // NB, n % NB
                dve.wait_ge(relu_ready, SLOTS * c + n + 1)
                for k in range(ON_ACT, BJ):
                    nc.vector.tensor_scalar(mask[:, n % RING, k, :].bitcast(U8), s1_bc[:, h % HG, :],
                                            s2_neg[:, BJ * b + k, h:h + 1], float(ONE8),
                                            ALU.is_gt, ALU.mult).then_inc(cmp_ready, 1)
                if n > 0:
                    other_mask(c, n - 1)
                dve.wait_ge(cmp_ready, (BJ - ON_ACT) * (SLOTS * c + n + 1))
                m = V32(mask[:, n % RING, 0:BJ, :])
                nc.vector.tensor_tensor(m, m, V32(adj[:, BJ * b:BJ * (b + 1), :]), ALU.bitwise_and).then_inc(and_ready, 1)

            def other_mask(c, n):
                b = n % NB
                dve.wait_ge(and_ready, SLOTS * c + n + 1)
                nc.vector.tensor_tensor(V32(mask[:, n % RING, BJ, :]), V32(mask[:, n % RING, ODD, :]),
                                        V32(adj[:, BJ * b + ODD, :]), ALU.bitwise_xor).then_inc(mask_ready, 1)

            def take_sums(c, h):
                dve.wait_ge(batch_done, NB * (H * c + h + 1) + RING)
                for q in range(2):
                    last = nc.vector.tensor_reduce(
                        sums[:, 2 * q:2 * q + 2, h % HG, :],
                        bank[2 * (h % 2) + q][:, 0:2 * PARTS * Q2].rearrange("p (t r q) -> p t q r", t=2, r=PARTS),
                        axis=AX.X, op=ALU.add)
                last.then_inc(sums_free, 1)

            def take_av(c, p):
                g, t = p // TPC, p % TPC
                dve.wait_ge(av_ready, NT * c + p + 1)
                nc.vector.tensor_reduce(
                    av[:, g % 2, t],
                    bank[4 + p % 2][:, 0:HG * PARTS * Q].rearrange("p (h r q) -> p h q r", h=HG, r=PARTS),
                    axis=AX.X, op=ALU.add).then_inc(av_free, 1)

            def combine(c, g):
                n = C_ALL * (NG * c + g)
                a, u, v = av[:, g % 2], sums[:, :, :, 0:Q], sums[:, :, :, Q:Q2]
                ra, rc = (f[:, bass.ds(TPC * c, TPC), HG * g:HG * (g + 1)].unsqueeze(3).broadcast_to([P, TPC, HG, Q])
                          for f in (row_a, row_c))
                dve.wait_ge(sums_free, HG * (NG * c + g + 1) + 2)
                dve.sem_inc(held, 1)
                nc.vector.tensor_tensor(a, a, v, ALU.subtract).then_inc(comb, 1)
                nc.vector.tensor_tensor(u, u, ra, ALU.mult).then_inc(comb, 1)
                dve.wait_ge(comb, n + 1)
                nc.vector.tensor_tensor(a, a, rc, ALU.mult).then_inc(comb, 1)
                dve.wait_ge(comb, n + 3)
                nc.vector.tensor_tensor(a, a, u, ALU.add).then_inc(comb, 1)
                dve.wait_ge(comb, n + 4)
                nc.vector.reciprocal(rden[:], a[:, :, :, DH]).then_inc(comb, 1)
                dve.wait_ge(comb, n + 5)
                dve.wait_ge(tok_tr1, TPC * c + 1)
                nc.vector.tensor_tensor(hid[:, :, D // NG * g:D // NG * (g + 1)].rearrange("p t (h d) -> p t h d", d=DH),
                                        a[:, :, :, 0:DH], rden[:].unsqueeze(3).broadcast_to([P, TPC, HG, DH]),
                                        ALU.mult).then_inc(comb, 1)

            def token_z(T):
                dve.wait_ge(tok_proj, T + 1)
                nc.vector.tensor_tensor(z[:], PR[:], b_row[:], ALU.add).then_inc(tok_z, 1)
                dve.wait_ge(tok_z, Z_ALL * T + 1)
                nc.vector.tensor_scalar(ez[:], z[:], 0.0, None, ALU.min).then_inc(tok_z, 1)

            def token_x(T):
                n = X_ALL * T
                dve.wait_ge(tok_exp, T + 1)
                nc.vector.scalar_tensor_tensor(ez[:], z[:], 0.0, ez[:], ALU.max, ALU.add).then_inc(tok_x, 1)
                dve.wait_ge(tok_x, n + 1)
                dve.wait_ge(xt_in, 16 * (T + 1))
                nc.vector.scalar_tensor_tensor(xt[:], ez[:], -1.0, xt[:], ALU.add, ALU.add).then_inc(tok_x, 1)
                dve.wait_ge(tok_x, n + 2)
                nc.vector.bn_stats(bst[:], xt[:]).then_inc(tok_x, 1)
                dve.wait_ge(tok_x, n + 3)
                dve.sem_inc(held, 1)
                nc.vector.bn_aggr(mv[:], bst[:]).then_inc(tok_x, 1)
                dve.wait_ge(tok_x, n + 4)
                nc.vector.tensor_scalar(rs[:, 0:1], mv[:, 1:2], EPS, None, ALU.add).then_inc(tok_x, 1)

            def token_norm(T):
                n = N_ALL * T
                dve.wait_ge(tok_rs, T + 1)
                nc.vector.scalar_tensor_tensor(rs[:, 2:3], rs[:, 1:2], rs[:, 1:2], rs[:, 0:1],
                                               ALU.mult, ALU.mult).then_inc(tok_n, 1)
                dve.wait_ge(tok_n, n + 1)
                nc.vector.tensor_scalar(rs[:, 2:3], rs[:, 2:3], -0.5, 1.5, ALU.mult, ALU.add).then_inc(tok_n, 1)
                dve.wait_ge(tok_n, n + 2)
                nc.vector.tensor_tensor(rs[:, 3:4], rs[:, 1:2], rs[:, 2:3], ALU.mult).then_inc(tok_n, 1)
                dve.wait_ge(tok_n, n + 3)
                dve.wait_ge(tok_tr2, T + 1)
                nc.vector.tensor_scalar(xn[:], xt[:], mv[:, 0:1], rs[:, 3:4], ALU.subtract, ALU.mult).then_inc(tok_n, 1)

            def token_low(T):
                dve.wait_ge(tok_xh, T + 1)
                nc.vector.tensor_tensor(xl[:], TR[:].rearrange("p (k i) -> p k i", k=KT), xh[:].bitcast(F32),
                                        ALU.subtract).then_inc(tok_low, 1)

            def chunk(c):
                first = isinstance(c, int)
                T = TPC * (c - 1)
                if not first:
                    fix_adj(c)
                dve.wait_ge(adj_ok, 4 * (c + 1))
                for n in range(SLOTS):
                    if not (first and n == 0):
                        masks(c, n)
                    if n == SLOTS - 1:
                        other_mask(c, n)
                    if n + SLOTS in TAKE and not first:
                        take_sums(c - 1, TAKE[n + SLOTS])
                    if n in TAKE:
                        take_sums(c, TAKE[n])
                    if n in TAKE_AV:
                        take_av(c, TAKE_AV[n])
                    if n + SLOTS in COMBINE and not first:
                        combine(c - 1, COMBINE[n + SLOTS])
                    if n in COMBINE:
                        combine(c, COMBINE[n])
                    if not first:
                        if n in TOK_Z:
                            token_z(T + TOK_Z[n])
                        if n in TOK_X:
                            token_x(T + TOK_X[n])
                        if n in TOK_N:
                            token_norm(T + TOK_N[n])
                        if n in TOK_HL:
                            token_low(T + TOK_HL[n])
                    else:
                        if n in LOW:
                            uv_rest(LOW[n], True)
                        if n in REST:
                            uv_rest(REST[n], False)
                        if n in MAKE:
                            uv_make(MAKE[n])
                        if n == 0:
                            uv_rest(1, True)

            uv_make(0)
            fix_adj(0)
            uv_rest(0, False)
            uv_make(1)
            uv_rest(0, True)
            dve.wait_ge(adj_ok, 4)
            masks(0, 0)
            uv_rest(1, False)
            chunk(0)
            with dve.Fori(1, NC) as c:
                chunk(c)
            for h in (H - 2, H - 1):
                take_sums(NC - 1, h)
            combine(NC - 1, NG - 1)
            def split_lo(u, s, par):
                dve.wait_ge(w_hi_ok, u + 1)
                nc.vector.tensor_tensor(w_lo[par][:, s, :], w_raw[:, s, :], w_hi[par][:, s, :].bitcast(F32),
                                        ALU.subtract).then_inc(w_lo_ok, 1)


            def make_gates():
                G = [0]

                def gstep(ins):
                    ins.then_inc(gate_dve, 1)
                    G[0] += 1
                    dve.wait_ge(gate_dve, G[0])
                b8 = lambda r: top[:, r, :].unsqueeze(2).broadcast_to([P, NT, E])
                dve.wait_ge(const_ok, 1 + E)
                rk = rank[:].unsqueeze(1).broadcast_to([P, NT, E])
                dve.wait_ge(sc_ready, 1)
                gstep(nc.vector.tensor_copy(sc[:], bank[7][:, 0:NT * E].rearrange("p (t e) -> p t e", e=E)))
                gstep(nc.vector.tensor_reduce(top[:, 0, :], sc[:], axis=AX.X, op=ALU.max))
                for r, eq in ((0, eq1), (1, eq2)):
                    gstep(nc.vector.tensor_tensor(eq[:], sc[:], b8(r), ALU.is_equal))
                    gstep(nc.vector.tensor_tensor(eq[:], eq[:], rk, ALU.mult))
                    gstep(nc.vector.tensor_reduce(top[:, 3, :], eq[:], axis=AX.X, op=ALU.max))
                    gstep(nc.vector.tensor_tensor(eq[:], eq[:], b8(3), ALU.is_equal))
                    if r == 0:
                        gstep(nc.vector.scalar_tensor_tensor(sc[:], eq[:], -3.0e38, sc[:], ALU.mult, ALU.add))
                        gstep(nc.vector.tensor_reduce(top[:, 1, :], sc[:], axis=AX.X, op=ALU.max))
                gstep(nc.vector.tensor_tensor(top[:, 2, :], top[:, 1, :], top[:, 0, :], ALU.subtract))
                assert G[0] == GATE_EXP, G[0]
                dve.wait_ge(gate_exp, 1)
                gstep(nc.vector.tensor_scalar(top[:, 4, :], top[:, 2, :], 1.0, None, ALU.add))
                gstep(nc.vector.reciprocal(top[:, 4, :], top[:, 4, :]))
                gstep(nc.vector.tensor_tensor(top[:, 5, :], top[:, 2, :], top[:, 4, :], ALU.mult))
                gstep(nc.vector.tensor_tensor(eq1[:], eq1[:], b8(4), ALU.mult))
                gstep(nc.vector.tensor_tensor(eq2[:], eq2[:], b8(5), ALU.mult))
                gstep(nc.vector.tensor_tensor(gates[:], eq1[:], eq2[:], ALU.add))
                dve.wait_ge(acc_in, 16)

            def last_z_min(k):
                dve.wait_ge(last_proj, k + 1)
                nc.vector.tensor_tensor(z4[:, k, :], bank[4 + k][:], b_row[:], ALU.add).then_inc(last_z, 1)
                dve.wait_ge(last_z, 2 * k + 1)
                nc.vector.tensor_scalar(ez4[:, k, :], z4[:, k, :], 0.0, None, ALU.min).then_inc(last_z, 1)

            def last_x2(k):
                x2 = acc[:, T_LAST + k, :]
                dve.wait_ge(last_exp, k + 1)
                nc.vector.scalar_tensor_tensor(ez4[:, k, :], z4[:, k, :], 0.0, ez4[:, k, :],
                                               ALU.max, ALU.add).then_inc(last_x, 1)
                dve.wait_ge(last_x, 4 * k + 1)
                dve.wait_ge(last_in, 16)
                nc.vector.scalar_tensor_tensor(x2, ez4[:, k, :], -1.0, x2, ALU.add, ALU.add).then_inc(last_x, 1)
                dve.wait_ge(last_x, 4 * k + 2)
                nc.vector.bn_stats(bst4[:, k, :], x2).then_inc(last_x, 1)
                dve.wait_ge(last_x, 4 * k + 3)
                nc.vector.bn_aggr(mv4[:, k, :], bst4[:, k, :]).then_inc(last_x, 1)

            def last_norm():
                dve.wait_ge(last_x, 4 * TPC)
                nc.vector.tensor_scalar(rs4[:, 0, :], mv4[:, :, 1], EPS, None, ALU.add).then_inc(last_x, 1)
                dve.wait_ge(last_rs, 1)
                y, t = rs4[:, 1, :], rs4[:, 2, :]
                nc.vector.tensor_tensor(t, y, y, ALU.mult).then_inc(last_n, 1)
                dve.wait_ge(last_n, 1)
                nc.vector.scalar_tensor_tensor(t, t, -0.5, rs4[:, 0, :], ALU.mult, ALU.mult).then_inc(last_n, 1)
                dve.wait_ge(last_n, 2)
                nc.vector.scalar_tensor_tensor(rs4[:, 3, :], t, 1.5, y, ALU.add, ALU.mult).then_inc(last_n, 1)
                dve.wait_ge(last_n, 3)
                for k in range(TPC):
                    nc.vector.tensor_scalar(xn4[:, k, :], acc[:, T_LAST + k, :], mv4[:, k, 0:1], rs4[:, 3, k:k + 1],
                                            ALU.subtract, ALU.mult).then_inc(last_n, 1)

            def last_lows():
                for k in range(TPC):
                    dve.wait_ge(last_xh, k + 1)
                    o = slice(k * P, (k + 1) * P)
                    nc.vector.tensor_tensor(XL[C_LAST][:, :, o], bank[4 + k][:].rearrange("p (k i) -> p k i", k=KT),
                                            XH[C_LAST][:, :, o].bitcast(F32), ALU.subtract).then_inc(last_low, 1)

            def hidden(S, par):
                for ht in range(GH):
                    n = GH * S + ht
                    dve.wait_ge(silu_ready, n + 1)
                    dve.wait_ge(h2_ready, n + 1)
                    nc.vector.tensor_tensor(act_g[:, ht, :], act_s[:, ht, :], bank[2 * ht + 1][:],
                                            ALU.mult).then_inc(g_ready, 1)
                    dve.wait_ge(g_ready, n + 1 + GH)
                    dve.wait_ge(y_ready, TPC * (S + 1))
                    nc.vector.tensor_copy(h_hi[:, par, ht, :], act_g[:, ht, :]).then_inc(hi_done, 1)
                    dve.wait_ge(hi_done, n + 1)
                    nc.vector.tensor_tensor(h_lo[:, par, ht, :], act_g[:, ht, :], h_hi[:, par, ht, :].bitcast(F32),
                                            ALU.subtract).then_inc(hid_ready, 1)

            def take_y(S, c, e):
                for tt in range(TPC):
                    t = TPC * c + tt
                    dve.wait_ge(y_ready, TPC * S + tt + 1 + 2 * TPC)
                    nc.vector.scalar_tensor_tensor(acc[:, t, :], bank[4 + tt][:], gates[:, t, bass.ds(e, 1)],
                                                   acc[:, t, :], ALU.mult, ALU.add).then_inc(y_used, 1)

            for k in range(TPC):
                if k < GH:
                    split_lo(k, k, 0)
                last_z_min(k)
                if k > 0:
                    last_x2(k - 1)
            last_x2(TPC - 1)
            last_norm()
            hidden(0, 0)
            last_lows()

            def two_groups(i, last):
                for k in range(2 * NC):
                    grp = 2 * i + k // NC
                    S = 2 * NC * i + k
                    if not (last and k == 2 * NC - 1):
                        hidden(S + 1, (k + 1) % 2)
                    if isinstance(i, int) and S == 0:
                        make_gates()
                    take_y(S, k % NC, i // 2 if isinstance(i, int) else i // 2)
                    if k % NC < GH and not (last and k >= NC):
                        split_lo(GH * (grp + 1) + k % NC, k % NC, (k // NC + 1) % 2)

            two_groups(0, False)
            with dve.Fori(1, GROUPS // 2 - 1) as i:
                two_groups(i, False)
            two_groups(GROUPS // 2 - 1, True)

        @block.sync
        def _(sp):
            sp.sem_inc(x2_out, 16)
            sp.sem_inc(xhl_out, 16)
            xv = x.rearrange("(t p) d -> p t d", p=P)
            xtile = x.rearrange("(t p) d -> t p d", p=P)
            for i in range(4):
                sp.dma_start(xall[:, 4 * i:4 * i + 4, :], xv[:, 4 * i:4 * i + 4, :]).then_inc(x_in[i], 16)
                if i == 0:
                    sp.dma_start(a_rows[:, 0, :], a1.partition_broadcast(P)).then_inc(w_in, 16)
                    sp.dma_start(a_rows[:, 1, :], a2.partition_broadcast(P)).then_inc(w_in, 16)
                    sp.dma_start(w_seq[:], W_seq.rearrange("(k p) n -> p k n", p=P)).then_inc(w_in, 16)
                    sp.dma_start(wg[:], WgT.rearrange("(k p) e -> p k e", p=P)).then_inc(w_in, 16)
            sp.wait_ge(su_sTc, NC)
            sp.dma_start(s1_rows.rearrange("(c h) i -> h c i", h=H),
                         s21T[H:2 * H, :].rearrange("h (c i) -> h c i", c=NC)).then_inc(s1_out, 16)
            sp.wait_ge(s1_out, 16)
            sp.wait_ge(su_act, 4)
            sp.wait_ge(su_dve, SU_COLS[0])
            for hh in range(HG):
                sp.dma_start(s1_bc[:, hh, :], s1_rows[hh].partition_broadcast(P)).then_inc(s1_in[hh], 16)

            def load_xt(T):
                sp.wait_ge(x2_out, 16 * T + 16)
                sp.sem_inc(held, 1)
                sp.dma_start(xt[:], xtile[T]).then_inc(xt_in, 16)

            def store_x2(T):
                sp.wait_ge(tok_n, N_ALL * (T + 1))
                sp.sem_inc(held, 1)
                sp.dma_start(x2_dram[T], xt[:]).then_inc(x2_out, 16)

            def store_hl(T, c, k):
                sp.wait_ge(tok_xh, T + 1)
                sp.sem_inc(held, 1)
                sp.wait_ge(tok_low, T + 1)
                sp.sem_inc(held, 1)
                sp.dma_start(xh_dram[c, :, :, k * P:(k + 1) * P], xh[:].bitcast(F32)).then_inc(xhl_out, 16)
                sp.dma_start(xl_dram[c, :, :, k * P:(k + 1) * P], xl[:].bitcast(F32)).then_inc(xhl_out, 16)

            def chunk(c):
                first = isinstance(c, int)
                T = TPC * (c - 1)
                if not first:
                    load_xt(T)
                for h in range(H):
                    sp.wait_ge(mask_ready, SLOTS * c + NB * (h + 1))
                    sp.sem_inc(held, 1)
                    row = (H * c + h + HG) % (NC * H) if h >= H - HG else H * c + h + HG
                    sp.dma_start(s1_bc[:, h % HG, :], s1_rows[row].partition_broadcast(P)).then_inc(s1_in[h % HG], 16)
                    for n in range(NB * h, NB * (h + 1)):
                        if not first and n in TOK_N:
                            store_x2(T + TOK_N[n])
                            if TOK_N[n] < TPC - 1:
                                load_xt(T + TOK_N[n] + 1)
                        if not first and n in TOK_HL:
                            store_hl(T + TOK_HL[n], c - 1, TOK_HL[n])
                if first:
                    sp.wait_ge(uv_ready, UPG * NG)
                    sp.dma_start(w_out[:], W_out.rearrange("(k p) n -> p k n", p=P)).then_inc(wo_in, 16)
                    sp.dma_start(b_row[:], b_out.partition_broadcast(P)).then_inc(wo_in, 16)

            chunk(0)
            with sp.Fori(1, NC) as c:
                chunk(c)
            sp.wait_ge(x2_out, 16 * T_LAST + 16)
            sp.wait_ge(xhl_out, 32 * T_LAST + 16)
            for u in range(GH):
                sp.dma_start(w_raw[:, u, :], ffn_w[u]).then_inc(raw_in[u], 16)
            sp.wait_ge(comb, HIDDEN_DONE)
            sp.wait_ge(adj_in, 64 * (NC + 1))
            for i in range(HG):
                sp.wait_ge(s1_in[i], 16 * (NC * H // HG + 1))
            sp.dma_start(acc[:, T_LAST:, :], xv[:, T_LAST:, :]).then_inc(last_in, 16)
            for c in range(C_LAST):
                sp.dma_start(XH[c][:].bitcast(F32), xh_dram[c]).then_inc(XT_in[c], 16)
                sp.dma_start(XL[c][:].bitcast(F32), xl_dram[c]).then_inc(XT_in[c], 16)
            sp.dma_start(acc[:, 0:T_LAST, :], x2_dram.rearrange("t p d -> p t d")).then_inc(acc_in, 16)
            with sp.Fori(1, UN // 2) as i:
                for s in range(2):
                    sp.wait_ge(w_hi_ok, 2 * i + s - 1)
                    sp.wait_ge(w_lo_ok, 2 * i + s - 1)
                    sp.sem_inc(held, 1)
                    sp.dma_start(w_raw[:, s, :], ffn_w[2 * i + s]).then_inc(raw_in[s], 16)
            ov = out.rearrange("(t p) d -> p t d", p=P)
            for t in range(NT):
                sp.wait_ge(y_used, TPC * NC * (GROUPS - 1) + t + 1 + TPC)
                sp.dma_start(ov[:, t, :], acc[:, t, :]).then_inc(out_done, 16)
            sp.wait_ge(out_done, 16 * NT)

        @block.gpsimd
        def _(pool):
            adj_v = adjT.rearrange("(j p) i -> p j i", p=P)

            def load_adj(c):
                for q in range(4):
                    pool.dma_start(adj_next[:, 4 * q:4 * q + 4, :],
                                   adj_v[:, 4 * q:4 * q + 4, c * CH:(c + 1) * CH]).then_inc(adj_in, 16)

            nc.gpsimd.memset(ident[:], 0.0).then_inc(su_pool, 1)
            nc.gpsimd.memset(ones[:], 1.0).then_inc(su_pool, 1)
            nc.gpsimd.memset(ones_bf[:], 1.0).then_inc(su_pool, 1)
            nc.gpsimd.memset(minus_half[:], -0.5).then_inc(su_pool, 1)
            pool.wait_ge(su_pool, 4)
            nc.gpsimd.affine_select(out=ident[:], in_=ident[:], compare_op=ALU.not_equal, fill=1.0, base=0,
                                    pattern=[[-1, P]], channel_multiplier=1).then_inc(const_ok, 1)
            for q in range(4):
                pool.wait_ge(su_dve, SU_VAR[q])
                nc.gpsimd.tensor_tensor(rs0[:, 1, 4 * q:4 * q + 4], rs0[:, 0, 4 * q:4 * q + 4],
                                        minus_half[:, 0:4], ALU.pow).then_inc(su_pool, 1)
                if q == 0:
                    load_adj(0)

            def rsqrt(T):
                pool.wait_ge(tok_x, X_ALL * (T + 1))
                nc.gpsimd.tensor_tensor(rs[:, 1:2], rs[:, 0:1], minus_half[:, 0:1], ALU.pow).then_inc(tok_rs, 1)

            for c in range(NC):
                pool.wait_ge(adj_ok, 4 * (c + 1))
                load_adj((c + 1) % NC)
                if c > 0:
                    with pool.Fori(TPC * (c - 1), TPC * c) as T:
                        rsqrt(T)
            pool.wait_ge(last_x, LAST_VAR)
            nc.gpsimd.tensor_tensor(rs4[:, 1, :], rs4[:, 0, :], minus_half[:], ALU.pow).then_inc(last_rs, 1)
            for e in range(E):
                nc.gpsimd.memset(rank[:, e:e + 1], float(E - e)).then_inc(const_ok, 1)

        @block.scalar
        def _(act):
            for t in range(NT):
                act.wait_ge(su_tr, t + 1)
                nc.scalar.copy(xT[:, :, t * P:(t + 1) * P],
                               bank[t % 2][:].rearrange("p (k i) -> p k i", k=KT)).then_inc(su_xT, 1)
                if t % TPC == TPC - 1:
                    c = t // TPC
                    act.wait_ge(su_sT, c + 1)
                    nc.scalar.copy(s21T[:, c * CH:(c + 1) * CH], bank[4 + c % 2][0:2 * H, :]).then_inc(su_sTc, 1)
            act.wait_ge(su_dve, SU_COLS[0])
            nc.scalar.activation(col_B[:], s2c[:], ACT.Exp).then_inc(su_act, 1)
            nc.scalar.activation(col_D[:], s2c[:], ACT.Exp, scale=0.2).then_inc(su_act, 1)
            nc.scalar.activation(row_a[:], ylo[:], ACT.Exp, scale=0.8).then_inc(su_act, 1)
            nc.scalar.activation(row_c[:], y_col[:], ACT.Exp, scale=-0.8).then_inc(su_act, 1)

            def uv_part(n, k):
                act.wait_ge(rest_ready if k else seq_used, n + 1)
                nc.scalar.copy(uv[:, unit(n)[0], unit(n)[1], k * Q2:(k + 1) * Q2],
                               uvf[:, n % 2]).then_inc(mid_ready if k else hi_ready, 1)

            def relus(c, n):
                h, b = n // NB, n % NB
                if b == 0:
                    act.wait_ge(s1_in[h % HG], 16 * (NG * c + h // HG + 1))
                act.wait_ge(batch_done, SLOTS * c + n + 1)
                act.sem_inc(held, 1)
                for k in range(ON_ACT):
                    last = nc.scalar.activation(mask[:, n % RING, k, :], s1_bc[:, h % HG, :], ACT.Relu, scale=BIG,
                                                bias=s2_big[:, BJ * b + k, h:h + 1], saturate=False)
                last.then_inc(relu_ready, 1)

            def hidT_copy(T, k):
                act.wait_ge(tok_tr1, T + 2)
                nc.scalar.copy(hidT[:, k], (TR, PR)[k % 2][:].rearrange("p (k i) -> p k i", k=KT)).then_inc(tok_hidT, 1)

            def elu_exp(T):
                act.wait_ge(tok_z, Z_ALL * (T + 1))
                nc.scalar.activation(ez[:], ez[:], ACT.Exp).then_inc(tok_exp, 1)

            def xh_copy(T):
                act.wait_ge(tok_tr2, T + 2)
                act.wait_ge(xhl_out, 32 * T + 16)
                nc.scalar.copy(xh[:], TR[:].rearrange("p (k i) -> p k i", k=KT)).then_inc(tok_xh, 1)

            def chunk(c):
                first = isinstance(c, int)
                T = TPC * (c - 1)
                for n in range(SLOTS):
                    if not (first and n < 3):
                        relus(c, n)
                    if not first:
                        if n in HIDT:
                            hidT_copy(T + HIDT[n], HIDT[n])
                        if n in TOK_EXP:
                            elu_exp(T + TOK_EXP[n])
                        if n in TOK_HL:
                            xh_copy(T + TOK_HL[n])
                    else:
                        if n in MID:
                            uv_part(MID[n], 1)
                        if n in HI:
                            uv_part(HI[n], 0)

            for n in range(2):
                uv_part(n, 0)
                relus(0, n)
                uv_part(n, 1)
            relus(0, 2)
            chunk(0)
            with act.Fori(1, NC) as c:
                chunk(c)
            def split_hi(grp, s, par):
                act.wait_ge(raw_in[s], 16 * (grp + 1))
                if not isinstance(grp, int) or grp > 0:
                    act.wait_ge(y_ready, TPC * NC * (grp - 1) + 2 * TPC)
                nc.scalar.copy(w_hi[par][:, s, :], w_raw[:, s, :]).then_inc(w_hi_ok, 1)

            def silu(S):
                for ht in range(GH):
                    n = GH * S + ht
                    act.wait_ge(h1_ready, n + 1)
                    act.wait_ge(g_ready, n + 1)
                    nc.scalar.activation(act_s[:, ht, :], bank[2 * ht][:], ACT.Silu).then_inc(silu_ready, 1)

            for k in range(TPC):
                act.wait_ge(last_tr1, k + 1)
                nc.scalar.copy(hidT[:, k], bank[4 + k][:].rearrange("p (k i) -> p k i", k=KT)).then_inc(last_hidT, 1)
            for i in range(HG):
                act.wait_ge(s1_in[i], 16 * (NC * H // HG + 1))
            for u in range(GH):
                split_hi(0, u, 0)
            for k in range(TPC):
                act.wait_ge(last_z, 2 * (k + 1))
                nc.scalar.activation(ez4[:, k, :], ez4[:, k, :], ACT.Exp).then_inc(last_exp, 1)

            def keep_scores(c):
                act.wait_ge(row_ready, c + 1)
                nc.scalar.copy(scT[:, c * CH:(c + 1) * CH], bank[4 + c % 2][0:E, :]).then_inc(row_kept, 1)

            silu(0)
            for c in range(2):
                keep_scores(c)
            for k in range(TPC):
                act.wait_ge(last_tr2, k + 1)
                nc.scalar.copy(XH[C_LAST][:, :, k * P:(k + 1) * P],
                               bank[4 + k][:].rearrange("p (k i) -> p k i", k=KT)).then_inc(last_xh, 1)

            def two_groups(i, last):
                for k in range(2 * NC):
                    grp = 2 * i + k // NC
                    S = 2 * NC * i + k
                    if not (last and k == 2 * NC - 1):
                        silu(S + 1)
                    if isinstance(i, int) and S == 0:
                        for c in range(2, NC):
                            keep_scores(c)
                        act.wait_ge(gate_dve, GATE_EXP)
                        nc.scalar.activation(top[:, 2, :], top[:, 2, :], ACT.Exp).then_inc(gate_exp, 1)
                    if k % NC < GH and not (last and k >= NC):
                        split_hi(grp + 1, k % NC, (k // NC + 1) % 2)

            two_groups(0, False)
            with act.Fori(1, GROUPS // 2 - 1) as i:
                two_groups(i, False)
            two_groups(GROUPS // 2 - 1, True)

        @block.tensor
        def _(pe):
            mm = nc.tensor.matmul
            pe.sem_inc(batch_done, RING)
            pe.sem_inc(sums_free, 2)
            pe.sem_inc(av_free, 2)
            pe.sem_inc(tok_tr1, 1)
            pe.sem_inc(tok_tr2, 1)
            pe.sem_inc(g_ready, GH)
            pe.sem_inc(y_ready, 2 * TPC)
            pe.sem_inc(y_used, TPC)

            pe.wait_ge(const_ok, 1)

            def project_seq(n):
                g, q = n // UPG, n % UPG
                if g > 0:
                    pe.wait_ge(seq_used, n - 1 if n >= UPG + 2 else 2)
                for i in range(UT):
                    t = UT * q + i
                    for k in range(KT):
                        last = mm(seq_bank(n)[:, i * P:(i + 1) * P], xT[:, k, t * P:(t + 1) * P],
                                  w_seq[:, k, g * P:(g + 1) * P], start=(k == 0), stop=(k == KT - 1))
                last.then_inc(seq_ready, 1)

            def score_rows(c):
                pe.wait_ge(su_dve, SU_W12[0])
                if c >= 2:
                    pe.wait_ge(su_sTc, c - 1)
                for k in range(KT):
                    last = mm(bank[4 + c % 2][0:2 * H, :], w12[:, k, :], xT[:, k, c * CH:(c + 1) * CH],
                              start=(k == 0), stop=(k == KT - 1))
                last.then_inc(su_sT, 1)

            pe.wait_ge(w_in, 64)
            for t in range(NT):
                pe.wait_ge(su_dve, SU_XN[t])
                if t >= 2:
                    pe.wait_ge(su_xT, t - 1)
                for k in range(KT):
                    last = nc.tensor.transpose(bank[t % 2][:, k * P:(k + 1) * P], xall[:, t, k * P:(k + 1) * P], ident[:])
                last.then_inc(su_tr, 1)
                if t % TPC == TPC - 1:
                    c = t // TPC
                    pe.wait_ge(su_xT, t + 1)
                    if c == 0:
                        project_seq(c)
                    score_rows(c)
                    if c == 1:
                        project_seq(c)
            project_seq(2)
            pe.wait_ge(su_sTc, NC)
            for t in range(NT):
                last = nc.tensor.transpose(bank[0][:, t * 2 * H:(t + 1) * 2 * H], s21T[:, t * P:(t + 1) * P],
                                           ident[0:2 * H, 0:2 * H])
            last.then_inc(su_cols, 1)
            pe.wait_ge(su_dve, SU_DIAG[0])
            mm(bank[1][:, 0:H], ones[0:H, :], gdiag[:], start=True, stop=True).then_inc(su_g, 1)

            def degrees(c):
                pe.wait_ge(adj_in, 64 * (c + 1))
                pe.sem_inc(held, 1)
                for j in range(NT):
                    last = mm(PR[:], ones_bf[:], adj_next[:, j, :], start=(j == 0), stop=(j == NT - 1))
                last.then_inc(deg_ready, 1)

            def head_batch(c, n):
                h, b = n // NB, n % NB
                if b == 0:
                    pe.wait_ge(sums_free, H * c + h + 1)
                pe.wait_ge(mask_ready, SLOTS * c + n + 1)
                pe.sem_inc(held, 1)
                for k in range(BJ):
                    j = BJ * b + k
                    for t in range(TPC):
                        o = (t % 2) * PARTS * Q2
                        out_ = bank[2 * (h % 2) + t // 2][:, o:o + PARTS * Q2]
                        ts = slice(t * P, (t + 1) * P)
                        if k != ODD:
                            mm(out_, mask[:, n % RING, k, ts], uv[:, j, h, :],
                               start=(j == 0 and t % 2 == 0), stop=False, skip_group_check=True)
                            continue
                        for s in range(2):
                            qs = slice(s * Q, (s + 1) * Q)
                            last = mm(out_.rearrange("p (r q) -> p r q", r=PARTS)[:, :, qs],
                                      mask[:, n % RING, ODD + s, ts],
                                      uv[:, j, h, :].rearrange("p (r q) -> p r q", r=PARTS)[:, :, qs],
                                      start=False, stop=(j == NT - 1), skip_group_check=True)
                last.then_inc(batch_done, 1)

            def adj_v(c, n):
                for m in range(AV_FROM[n], AV_FROM[n + 1]):
                    p, i = m // AVJ, m % AVJ
                    j = BJ * (i // ODD) + i % ODD
                    g, t = p // TPC, p % TPC
                    if i == 0:
                        pe.wait_ge(av_free, NT * c + p + 1)
                        pe.sem_inc(held, 1)
                        if t == 0 and g > 0 and isinstance(c, int):
                            pe.wait_ge(uv_ready, UPG * (g + 1))
                        if p == 1 and isinstance(c, int):
                            pe.wait_ge(seq_used, UPG)
                    if p == 0 and j % UT == 0 and isinstance(c, int):
                        pe.wait_ge(uv_ready, j // UT + 1)
                    rhs = uv[:, j, HG * g:HG * (g + 1), :].rearrange("p h (r q) -> p h r q", r=PARTS)[:, :, :, Q:Q2]
                    mm_ = mm(bank[4 + p % 2][:, 0:HG * PARTS * Q], adj[:, j, t * P:(t + 1) * P], rhs,
                             start=(i == 0), stop=(i == AVJ - 1))
                    if i == AVJ - 1:
                        mm_.then_inc(av_ready, 1)

            def tok_transpose(T, k):
                if k >= 2:
                    pe.wait_ge(tok_hidT, T - 1)
                for q in range(KT):
                    last = nc.tensor.transpose((TR, PR)[k % 2][:, q * P:(q + 1) * P], hid[:, k, q * P:(q + 1) * P], ident[:])
                last.then_inc(tok_tr1, 1)

            def tok_project(T, k):
                for q in range(KT):
                    last = mm(PR[:], hidT[:, k, q, :], w_out[:, q, :], start=(q == 0), stop=(q == KT - 1))
                last.then_inc(tok_proj, 1)

            def tok_transpose2(T):
                pe.wait_ge(tok_n, N_ALL * (T + 1))
                for k in range(KT):
                    last = nc.tensor.transpose(TR[:, k * P:(k + 1) * P], xn[:, k * P:(k + 1) * P], ident[:])
                last.then_inc(tok_tr2, 1)

            def chunk(c):
                first = isinstance(c, int)
                T = TPC * (c - 1)
                pe.wait_ge(adj_ok, 4 * (c + 1))
                for n in range(SLOTS):
                    if first and n < UPG:
                        pe.wait_ge(uv_ready, n + 1)
                    elif first and n % (NB * HG) == 0:
                        pe.wait_ge(uv_ready, UPG * (n // (NB * HG) + 1))
                    if first and n == NB:
                        pe.wait_ge(seq_used, UPG)
                    head_batch(c, n)
                    if first and n in SEQ:
                        project_seq(SEQ[n])
                    adj_v(c, n)
                    if not first:
                        if n in TR1:
                            if TR1[n] == 0:
                                pe.wait_ge(comb, C_ALL * NG * c)
                            tok_transpose(T + TR1[n], TR1[n])
                        if n in PROJ:
                            if PROJ[n] == 0:
                                pe.wait_ge(tok_hidT, T + TPC)
                            else:
                                pe.wait_ge(tok_z, Z_ALL * (T + PROJ[n]))
                            tok_project(T, PROJ[n])
                        if n in TR2:
                            if TR2[n] > 0:
                                pe.wait_ge(tok_low, T + TR2[n])
                            tok_transpose2(T + TR2[n])
                    if n == DEGREES:
                        if not first:
                            pe.wait_ge(tok_z, Z_ALL * (T + TPC))
                        degrees(c + 1)
                if first:
                    pe.wait_ge(wo_in, 32)

            degrees(0)
            project_seq(UPG - 1)
            pe.wait_ge(empty_ready, 1)
            for n in range(UPG, UPG + 2):
                project_seq(n)
            chunk(0)
            with pe.Fori(1, NC) as c:
                chunk(c)
            def three(out_, hi, lo, rhi, rlo, start, stop):
                mm(out_, hi, rhi, start=start, stop=False)
                mm(out_, hi, rlo, start=False, stop=False)
                return mm(out_, lo, rhi, start=False, stop=stop)

            def up(S, grp, par, c):
                if c == 0:
                    pe.wait_ge(w_hi_ok, GH * (grp + 1))
                    pe.wait_ge(w_lo_ok, GH * (grp + 1))
                if c < C_LAST:
                    pe.wait_ge(XT_in[c], 32)
                for ht in range(GH):
                    pe.wait_ge(g_ready, GH * S + ht + 1)
                    for s, done in ((0, h1_ready), (1, h2_ready)):
                        for k in range(KT):
                            o = s * D + k * P
                            last = three(bank[2 * ht + s][:], w_hi[par][:, ht, o:o + P], w_lo[par][:, ht, o:o + P],
                                         XH[c][:, k, :], XL[c][:, k, :], k == 0, k == KT - 1)
                        last.then_inc(done, 1)

            def down(S, grp, par, hpar, c):
                pe.wait_ge(hid_ready, GH * (S + 1))
                for tt in range(TPC):
                    pe.wait_ge(y_used, TPC * S + tt + 1)
                    if isinstance(S, int) and S == 0 and tt == TPC - 1:
                        pe.wait_ge(gate_dve, 1)
                    for ht in range(GH):
                        last = three(bank[4 + tt][:], h_hi[:, hpar, ht, tt * P:(tt + 1) * P],
                                     h_lo[:, hpar, ht, tt * P:(tt + 1) * P],
                                     w_hi[par][:, ht, 2 * D:], w_lo[par][:, ht, 2 * D:], ht == 0, ht == GH - 1)
                    last.then_inc(y_ready, 1)

            def score_rows_of(c):
                if c < C_LAST:
                    pe.wait_ge(XT_in[c], 32)
                    pe.wait_ge(last_z, 2 * (c % 2 + 1))
                else:
                    pe.wait_ge(last_low, TPC)
                if c >= 2:
                    pe.wait_ge(last_low, c % 2 + 1)
                for k in range(KT):
                    last = three(bank[4 + c % 2][0:E, :], wg_hi[:, k, :], wg_lo[:, k, :],
                                 XH[c][:, k, :], XL[c][:, k, :], k == 0, k == KT - 1)
                last.then_inc(row_ready, 1)

            def score_columns():
                pe.wait_ge(last_low, TPC)
                pe.wait_ge(row_kept, NC)
                for t in range(NT):
                    last = nc.tensor.transpose(bank[7][:, t * E:(t + 1) * E], scT[:, t * P:(t + 1) * P], ident[0:E, 0:E])
                last.then_inc(sc_ready, 1)

            pe.wait_ge(comb, HIDDEN_DONE)
            for k in range(TPC):
                for q in range(KT):
                    last = nc.tensor.transpose(bank[4 + k][:, q * P:(q + 1) * P], hid[:, k, q * P:(q + 1) * P], ident[:])
                last.then_inc(last_tr1, 1)
            for k in range(TPC):
                pe.wait_ge(last_hidT, k + 1)
                for q in range(KT):
                    last = mm(bank[4 + k][:], hidT[:, k, q, :], w_out[:, q, :], start=(q == 0), stop=(q == KT - 1))
                last.then_inc(last_proj, 1)
            up(0, 0, 0, 0)
            score_rows_of(0)
            score_rows_of(1)
            for k in range(TPC):
                pe.wait_ge(last_n, 3 + k + 1)
                if k < 2:
                    pe.wait_ge(row_kept, k + 1)
                for q in range(KT):
                    last = nc.tensor.transpose(bank[4 + k][:, q * P:(q + 1) * P], xn4[:, k, q * P:(q + 1) * P], ident[:])
                last.then_inc(last_tr2, 1)

            def two_groups(i, last):
                for k in range(2 * NC):
                    grp = 2 * i + k // NC
                    S = 2 * NC * i + k
                    if not (last and k == 2 * NC - 1):
                        k1 = k + 1
                        up(S + 1, 2 * i + k1 // NC, (k1 // NC) % 2, k1 % NC)
                    if isinstance(i, int) and S == 0:
                        score_rows_of(2)
                        score_rows_of(3)
                        score_columns()
                    down(S, grp, (k // NC) % 2, k % 2, k % NC)

            two_groups(0, False)
            with pe.Fori(1, GROUPS // 2 - 1) as i:
                two_groups(i, False)
            two_groups(GROUPS // 2 - 1, True)


def kernel(**inputs):
    import numpy as np
    import concourse.bacc as bacc
    from concourse.bass_utils import run_bass_kernel_spmd

    a = {k: np.asarray(v) for k, v in inputs.items()}

    def up_layout(w):
        return w.reshape(E, HID // P, P, KT, P).transpose(0, 1, 4, 3, 2).reshape(UN, P, D)

    w3 = a["L0_ffn_W3"].reshape(E, D, HID // P, P).transpose(0, 2, 3, 1).reshape(UN, P, D)
    arrays = {
        "x": a["x"], "adjT": a["adj"].T, "W_seq": a["L0_gnn_W_seq"], "a1": a["L0_gnn_a1"], "a2": a["L0_gnn_a2"],
        "W_out": a["L0_gnn_W_out"], "b_out": a["L0_gnn_b_out"], "WgT": a["L0_ffn_Wg"].T,
        "ffn_w": np.concatenate([up_layout(a["L0_ffn_W1"]), up_layout(a["L0_ffn_W2"]), w3], axis=2),
    }
    arrays = {k: np.ascontiguousarray(v) for k, v in arrays.items()}
    nc = bacc.Bacc("TRN2", target_bir_lowering=False, num_devices=1, dynamic_dma_scratch_size=4096)
    args = [nc.dram_tensor(k, v.shape, mybir.dt.from_np(v.dtype), kind="ExternalInput").ap() for k, v in arrays.items()]
    args.append(nc.dram_tensor("out", (N, D), F32, kind="ExternalOutput").ap())
    build(nc, *args)
    r = run_bass_kernel_spmd(nc, [arrays], core_ids=[0])
    return r.results[0]["out"]
```
